# Optimizing a Trainium2 kernel written in Bass

```python
import numpy as np
import jax
import jax.numpy as jnp

def _softmax(x, axis=-1):
    return jax.nn.softmax(x, axis=axis)

def _gelu(x):
    return jax.nn.gelu(x, approximate=True)

def _silu(x):
    return jax.nn.silu(x)

def _sigmoid(x):
    return jax.nn.sigmoid(x)

def _layernorm(x, axis=-1, eps=1e-05):
    m = jnp.mean(x, axis=axis, keepdims=True)
    v = jnp.var(x, axis=axis, keepdims=True)
    return (x - m) / jnp.sqrt(v + eps)

def _scatter_add(tgt, idx, src, axis=0):
    return tgt.at[idx].add(src)

def _segment_sum(src, seg, n):
    return jax.ops.segment_sum(src, seg, n)
kernel_name = 'mk_cond_seq_d4_seqx_r2_d945b5'

def setup_inputs(seed: int=0):
    np.random.seed(seed)
    _w = jnp.asarray

    def _rec_inputs():
        import jax
        import jax.numpy as jnp
        _rk = jax.random.key(seed)
        x = -0.000125 + 0.9999 * jax.random.normal(jax.random.fold_in(_rk, 1), (2, 2048, 512), jnp.float32)
        _lenS = 2048 - jax.random.randint(jax.random.fold_in(_rk, 7), (2,), 0, max(1, 2048 // 4) + 1, jnp.int32)
        _lenS2 = 2048 - jax.random.randint(jax.random.fold_in(_rk, 8), (2,), 0, max(1, 2048 // 4) + 1, jnp.int32)
        itok_B_0_15 = jax.random.randint(jax.random.fold_in(_rk, 11), (2,), 0, 16, jnp.int32)
        itok_B_34_63 = jax.random.randint(jax.random.fold_in(_rk, 13), (2,), 34, 64, jnp.int32)
        fside_Bx16xSxS_0 = -1.47943e-05 + 1.00017 * jax.random.normal(jax.random.fold_in(_rk, 14), (2, 16, 2048, 2048), jnp.float32)
        condB_theta = jax.random.uniform(jax.random.fold_in(_rk, 15), (2,), jnp.float32, 0.0, 0.983423)
        condB_phi = jax.random.uniform(jax.random.fold_in(_rk, 16), (2,), jnp.float32, 0.0, 0.961312)
        condB_safetyscore = -0.927215 + 0.920279 * jax.random.normal(jax.random.fold_in(_rk, 17), (2,), jnp.float32)
        _validS = jnp.arange(2048)[None, :] < _lenS[:, None]
        _validS2 = jnp.arange(2048)[None, :] < _lenS2[:, None]
        _causal = jnp.tril(jnp.ones((2048, 2048), dtype=bool))
        mask_Bx1xSxS_bk0 = jnp.logical_not(jnp.broadcast_to(_validS[:, None, None, :], (2, 1, 2048, 2048)))
        return (x, itok_B_0_15, itok_B_34_63, fside_Bx16xSxS_0, condB_theta, condB_phi, condB_safetyscore, mask_Bx1xSxS_bk0)
    x, itok_B_0_15, itok_B_34_63, fside_Bx16xSxS_0, condB_theta, condB_phi, condB_safetyscore, mask_Bx1xSxS_bk0 = _rec_inputs()

    def _L0_cond_setup():
        import jax, jax.numpy as jnp
        import numpy as np
        B, S, D = (32, 512, 512)
        A = 128
        E = 16
        LN_EPS = 1e-05
        key = jax.random.key(seed)
        ks = jax.random.split(key, 10)
        s = lambda fan_in: 1.0 / np.sqrt(fan_in)
        return {'hidden_states': jax.random.normal(ks[0], (B, S, D), dtype=jnp.float32), 'domain_id': jax.random.randint(ks[1], (B,), 0, E, dtype=jnp.int64), 'down_W': jax.random.uniform(ks[2], (A, D), jnp.float32, -s(D), s(D)), 'down_b': jax.random.uniform(ks[3], (A,), jnp.float32, -s(D), s(D)), 'up_W': jax.random.uniform(ks[4], (D, A), jnp.float32, -s(A), s(A)), 'up_b': jax.random.uniform(ks[5], (D,), jnp.float32, -s(A), s(A)), 'expert_W': jax.random.uniform(ks[6], (E, A, A), jnp.float32, -s(A), s(A)), 'expert_b': jax.random.uniform(ks[7], (E, A), jnp.float32, -s(A), s(A)), 'domain_emb': jax.random.normal(ks[8], (E, A), dtype=jnp.float32), 'ln_gamma': jnp.ones((D,), jnp.float32), 'ln_beta': jnp.zeros((D,), jnp.float32)}
    _L0_cond_all = _L0_cond_setup()
    _L0_cond_in = {k: v for k, v in _L0_cond_all.items() if k in ('down_W', 'down_b', 'up_W', 'up_b', 'expert_W', 'expert_b', 'domain_emb', 'ln_gamma', 'ln_beta')}
    del _L0_cond_all

    def _L1_cond_setup():
        import jax, jax.numpy as jnp
        import numpy as np
        import math
        D_MODEL = 512
        N_HEAD = 16
        HEAD_DIM = D_MODEL // N_HEAD
        D_FF = 2048
        NUM_STEPS = 100.0
        RESCALE = 4000.0
        EPS = 1e-05

        def _sin_emb(t):
            half = D_MODEL // 2
            x = t.astype(jnp.float32) / NUM_STEPS * RESCALE
            freqs = jnp.exp(jnp.arange(half, dtype=jnp.float32) * (-math.log(10000.0) / (half - 1)))
            e = x[:, None] * freqs[None, :]
            return jnp.concatenate([jnp.sin(e), jnp.cos(e)], axis=-1)

        def _ln(x):
            m = jnp.mean(x, axis=-1, keepdims=True)
            v = jnp.var(x, axis=-1, keepdims=True)
            return (x - m) / jnp.sqrt(v + EPS)

        def _gelu2(x):
            return x * jax.nn.sigmoid(1.702 * x)
        key = jax.random.key(seed)
        ks = jax.random.split(key, 24)
        B, S, D, F = (4, 256, D_MODEL, D_FF)
        std = 0.02
        inp = {'src': jax.random.normal(ks[0], (B, S, D), dtype=jnp.float32), 'src_mask': jax.random.randint(ks[1], (B, 1, S, S), 0, 2).astype(bool), 'timestep': jax.random.randint(ks[2], (B,), 0, 100, dtype=jnp.int32), 'attention_bias': jax.random.normal(ks[3], (B, N_HEAD, S, S), dtype=jnp.float32), 'W_ada': jax.random.normal(ks[4], (D, 2 * D), dtype=jnp.float32) * std, 'b_ada': jnp.zeros((2 * D,), dtype=jnp.float32), 'Wq': jax.random.normal(ks[5], (D, D), dtype=jnp.float32) * std, 'bq': jnp.zeros((D,), dtype=jnp.float32), 'Wk': jax.random.normal(ks[6], (D, D), dtype=jnp.float32) * std, 'bk': jnp.zeros((D,), dtype=jnp.float32), 'Wv': jax.random.normal(ks[7], (D, D), dtype=jnp.float32) * std, 'bv': jnp.zeros((D,), dtype=jnp.float32), 'Wo': jax.random.normal(ks[8], (D, D), dtype=jnp.float32) * std, 'bo': jnp.zeros((D,), dtype=jnp.float32), 'W1': jax.random.normal(ks[9], (D, F), dtype=jnp.float32) * std, 'b1': jnp.zeros((F,), dtype=jnp.float32), 'W2': jax.random.normal(ks[10], (F, D), dtype=jnp.float32) * std, 'b2': jnp.zeros((D,), dtype=jnp.float32), 'g2': jnp.ones((D,), dtype=jnp.float32), 'beta2': jnp.zeros((D,), dtype=jnp.float32)}
        return inp
    _L1_cond_all = _L1_cond_setup()
    _L1_cond_in = {k: v for k, v in _L1_cond_all.items() if k in ('W_ada', 'b_ada', 'Wq', 'bq', 'Wk', 'bk', 'Wv', 'bv', 'Wo', 'bo', 'W1', 'b1', 'W2', 'b2', 'g2', 'beta2')}
    del _L1_cond_all

    def _L2_cond_setup():
        import jax, jax.numpy as jnp
        import numpy as np
        key = jax.random.key(seed)
        k1, k2, k3 = jax.random.split(key, 3)
        B, N, D = (16, 2048, 512)
        embeddings = jax.random.normal(k1, (B, N, D), dtype=jnp.float32)
        theta = jax.random.uniform(k2, (B,), dtype=jnp.float32)
        phi = jax.random.uniform(k3, (B,), dtype=jnp.float32)
        return {'embeddings': embeddings, 'theta': theta, 'phi': phi}
    _L2_cond_all = _L2_cond_setup()
    _L2_cond_in = {k: v for k, v in _L2_cond_all.items() if k in ()}
    del _L2_cond_all

    def _L3_cond_setup():
        import jax, jax.numpy as jnp
        import numpy as np
        TEMPERATURE = 1.0
        ACT_THRESHOLD = 0.1
        MAX_ACT = 1.0
        SAFETY_KNOB = 1.0
        EPS = 1e-08

        def gram_schmidt(X):
            r = X.shape[1]
            Q = X
            for i in range(r):
                q = Q[:, i]
                q = q / (jnp.linalg.norm(q) + EPS)
                Q = Q.at[:, i].set(q)
                coeffs = q @ Q[:, i + 1:]
                Q = Q.at[:, i + 1:].add(-jnp.outer(q, coeffs))
            return Q
        key = jax.random.key(seed)
        ks = jax.random.split(key, 8)
        B, S, D, R = (8, 2048, 512, 32)
        init_std = 0.02
        return {'hidden_states': jax.random.normal(ks[0], (B, S, D), jnp.float32), 'safety_score': jax.random.normal(ks[1], (B,), jnp.float32), 'U': jax.random.normal(ks[2], (D, R), jnp.float32) * init_std, 'V': jax.random.normal(ks[3], (D, R), jnp.float32) * init_std, 'safety_bias': jnp.zeros((D,), jnp.float32), 'gate_w1': jax.random.normal(ks[4], (D // 4, D), jnp.float32) * (1.0 / np.sqrt(D)), 'gate_b1': jnp.zeros((D // 4,), jnp.float32), 'gate_w2': jax.random.normal(ks[5], (1, D // 4), jnp.float32) * (1.0 / np.sqrt(D // 4)), 'gate_b2': jnp.zeros((1,), jnp.float32), 'resp_w': jax.random.normal(ks[6], (D, R), jnp.float32) * (1.0 / np.sqrt(R)), 'resp_b': jnp.zeros((D,), jnp.float32)}
    _L3_cond_all = _L3_cond_setup()
    _L3_cond_in = {k: v for k, v in _L3_cond_all.items() if k in ('U', 'V', 'safety_bias', 'gate_w1', 'gate_b1', 'gate_w2', 'gate_b2', 'resp_w', 'resp_b')}
    del _L3_cond_all
    return {'x': x, 'itok_B_0_15': itok_B_0_15, 'itok_B_34_63': itok_B_34_63, 'fside_Bx16xSxS_0': fside_Bx16xSxS_0, 'condB_theta': condB_theta, 'condB_phi': condB_phi, 'condB_safetyscore': condB_safetyscore, 'mask_Bx1xSxS_bk0': mask_Bx1xSxS_bk0, 'L0_cond_down_W': _L0_cond_in['down_W'], 'L0_cond_down_b': _L0_cond_in['down_b'], 'L0_cond_up_W': _L0_cond_in['up_W'], 'L0_cond_up_b': _L0_cond_in['up_b'], 'L0_cond_expert_W': _L0_cond_in['expert_W'], 'L0_cond_expert_b': _L0_cond_in['expert_b'], 'L0_cond_domain_emb': _L0_cond_in['domain_emb'], 'L0_cond_ln_gamma': _L0_cond_in['ln_gamma'], 'L0_cond_ln_beta': _L0_cond_in['ln_beta'], 'L1_cond_W_ada': _L1_cond_in['W_ada'], 'L1_cond_b_ada': _L1_cond_in['b_ada'], 'L1_cond_Wq': _L1_cond_in['Wq'], 'L1_cond_bq': _L1_cond_in['bq'], 'L1_cond_Wk': _L1_cond_in['Wk'], 'L1_cond_bk': _L1_cond_in['bk'], 'L1_cond_Wv': _L1_cond_in['Wv'], 'L1_cond_bv': _L1_cond_in['bv'], 'L1_cond_Wo': _L1_cond_in['Wo'], 'L1_cond_bo': _L1_cond_in['bo'], 'L1_cond_W1': _L1_cond_in['W1'], 'L1_cond_b1': _L1_cond_in['b1'], 'L1_cond_W2': _L1_cond_in['W2'], 'L1_cond_b2': _L1_cond_in['b2'], 'L1_cond_g2': _L1_cond_in['g2'], 'L1_cond_beta2': _L1_cond_in['beta2'], 'L3_cond_U': _L3_cond_in['U'], 'L3_cond_V': _L3_cond_in['V'], 'L3_cond_safety_bias': _L3_cond_in['safety_bias'], 'L3_cond_gate_w1': _L3_cond_in['gate_w1'], 'L3_cond_gate_b1': _L3_cond_in['gate_b1'], 'L3_cond_gate_w2': _L3_cond_in['gate_w2'], 'L3_cond_gate_b2': _L3_cond_in['gate_b2'], 'L3_cond_resp_w': _L3_cond_in['resp_w'], 'L3_cond_resp_b': _L3_cond_in['resp_b']}

def reference(x, itok_B_0_15, itok_B_34_63, fside_Bx16xSxS_0, condB_theta, condB_phi, condB_safetyscore, mask_Bx1xSxS_bk0, L0_cond_down_W, L0_cond_down_b, L0_cond_up_W, L0_cond_up_b, L0_cond_expert_W, L0_cond_expert_b, L0_cond_domain_emb, L0_cond_ln_gamma, L0_cond_ln_beta, L1_cond_W_ada, L1_cond_b_ada, L1_cond_Wq, L1_cond_bq, L1_cond_Wk, L1_cond_bk, L1_cond_Wv, L1_cond_bv, L1_cond_Wo, L1_cond_bo, L1_cond_W1, L1_cond_b1, L1_cond_W2, L1_cond_b2, L1_cond_g2, L1_cond_beta2, L3_cond_U, L3_cond_V, L3_cond_safety_bias, L3_cond_gate_w1, L3_cond_gate_b1, L3_cond_gate_w2, L3_cond_gate_b2, L3_cond_resp_w, L3_cond_resp_b):
    import jax
    import jax.numpy as jnp

    def _L0_cond_ref(hidden_states, domain_id, down_W, down_b, up_W, up_b, expert_W, expert_b, domain_emb, ln_gamma, ln_beta):
        import jax, jax.numpy as jnp
        import numpy as np
        B, S, D = (32, 512, 512)
        A = 128
        E = 16
        LN_EPS = 1e-05
        residual = hidden_states
        hidden = jnp.einsum('bsd,ad->bsa', hidden_states, down_W) + down_b
        hidden = jax.nn.gelu(hidden, approximate=False)
        valid = (domain_id >= 0) & (domain_id < E)
        idx = jnp.clip(domain_id, 0, E - 1)
        Wsel = expert_W[idx]
        bsel = expert_b[idx]
        expert_out = jnp.einsum('bsa,boa->bso', hidden, Wsel) + bsel[:, None, :]
        domain_output = jnp.where(valid[:, None, None], expert_out, hidden)
        hidden = domain_output + domain_emb[idx][:, None, :]
        hidden = jnp.einsum('bsa,da->bsd', hidden, up_W) + up_b
        x = hidden + residual
        mu = jnp.mean(x, axis=-1, keepdims=True)
        var = jnp.mean(jnp.square(x - mu), axis=-1, keepdims=True)
        return (x - mu) * jax.lax.rsqrt(var + LN_EPS) * ln_gamma + ln_beta

    def _L1_cond_ref(src, src_mask, timestep, attention_bias, W_ada, b_ada, Wq, bq, Wk, bk, Wv, bv, Wo, bo, W1, b1, W2, b2, g2, beta2):
        import jax, jax.numpy as jnp
        import numpy as np
        import math
        D_MODEL = 512
        N_HEAD = 16
        HEAD_DIM = D_MODEL // N_HEAD
        D_FF = 2048
        NUM_STEPS = 100.0
        RESCALE = 4000.0
        EPS = 1e-05

        def _sin_emb(t):
            half = D_MODEL // 2
            x = t.astype(jnp.float32) / NUM_STEPS * RESCALE
            freqs = jnp.exp(jnp.arange(half, dtype=jnp.float32) * (-math.log(10000.0) / (half - 1)))
            e = x[:, None] * freqs[None, :]
            return jnp.concatenate([jnp.sin(e), jnp.cos(e)], axis=-1)

        def _ln(x):
            m = jnp.mean(x, axis=-1, keepdims=True)
            v = jnp.var(x, axis=-1, keepdims=True)
            return (x - m) / jnp.sqrt(v + EPS)

        def _gelu2(x):
            return x * jax.nn.sigmoid(1.702 * x)
        B, S, D = src.shape
        emb = jax.nn.silu(_sin_emb(timestep)) @ W_ada + b_ada
        scale, shift = jnp.split(emb[:, None, :], 2, axis=-1)
        x = _ln(src) * (1.0 + scale) + shift
        q = (x @ Wq + bq).reshape(B, S, N_HEAD, HEAD_DIM).transpose(0, 2, 1, 3)
        k = (x @ Wk + bk).reshape(B, S, N_HEAD, HEAD_DIM).transpose(0, 2, 1, 3)
        v = (x @ Wv + bv).reshape(B, S, N_HEAD, HEAD_DIM).transpose(0, 2, 1, 3)
        scores = jnp.einsum('bhqd,bhkd->bhqk', q / math.sqrt(HEAD_DIM), k)
        scores = scores + attention_bias
        scores = jnp.where(src_mask, -jnp.inf, scores.astype(jnp.float32))
        probs = jax.nn.softmax(scores, axis=-1).astype(v.dtype)
        ctx = jnp.einsum('bhqk,bhkd->bhqd', probs, v)
        ctx = ctx.transpose(0, 2, 1, 3).reshape(B, S, D)
        x = x + (ctx @ Wo + bo)
        h = _ln(x) * g2 + beta2
        ff = _gelu2(h @ W1 + b1) @ W2 + b2
        return x + ff

    def _L2_cond_ref(embeddings, theta, phi):
        import jax, jax.numpy as jnp
        import numpy as np
        B, N, D = embeddings.shape
        e = embeddings.reshape(B, N, D // 4, 4)
        ct = jnp.cos(theta)[:, None, None]
        st = jnp.sin(theta)[:, None, None]
        cp = jnp.cos(phi)[:, None, None]
        sp = jnp.sin(phi)[:, None, None]
        x0, x1, x2, x3 = (e[..., 0], e[..., 1], e[..., 2], e[..., 3])
        out = jnp.stack([x0 * ct + x1 * st, -x0 * st + x1 * ct, x2 * cp + x3 * sp, -x2 * sp + x3 * cp], axis=-1)
        return out.reshape(B, N, D)

    def _L3_cond_ref(hidden_states, safety_score, U, V, safety_bias, gate_w1, gate_b1, gate_w2, gate_b2, resp_w, resp_b):
        import jax, jax.numpy as jnp
        import numpy as np
        TEMPERATURE = 1.0
        ACT_THRESHOLD = 0.1
        MAX_ACT = 1.0
        SAFETY_KNOB = 1.0
        EPS = 1e-08

        def gram_schmidt(X):
            r = X.shape[1]
            Q = X
            for i in range(r):
                q = Q[:, i]
                q = q / (jnp.linalg.norm(q) + EPS)
                Q = Q.at[:, i].set(q)
                coeffs = q @ Q[:, i + 1:]
                Q = Q.at[:, i + 1:].add(-jnp.outer(q, coeffs))
            return Q
        R = resp_w.shape[1]
        U_o = gram_schmidt(U)
        V_o = gram_schmidt(V)
        basis = U_o @ V_o.T
        pooled = hidden_states.mean(axis=1)
        h1 = jax.nn.relu(pooled @ gate_w1.T + gate_b1)
        base_act = jax.nn.sigmoid(h1 @ gate_w2.T + gate_b2)
        mod = jax.nn.sigmoid(safety_score[:, None] / TEMPERATURE)
        knob = jnp.clip(jnp.asarray(SAFETY_KNOB, hidden_states.dtype), ACT_THRESHOLD, MAX_ACT)
        strength = (base_act * mod * knob)[:, None, :]
        proj = hidden_states @ basis
        feats = proj @ basis.T[:, :R]
        response = feats @ resp_w.T + resp_b + safety_bias
        return hidden_states + strength * response
    x = _L0_cond_ref(x, itok_B_0_15, L0_cond_down_W, L0_cond_down_b, L0_cond_up_W, L0_cond_up_b, L0_cond_expert_W, L0_cond_expert_b, L0_cond_domain_emb, L0_cond_ln_gamma, L0_cond_ln_beta)
    x = _L1_cond_ref(x, mask_Bx1xSxS_bk0, itok_B_34_63, fside_Bx16xSxS_0, L1_cond_W_ada, L1_cond_b_ada, L1_cond_Wq, L1_cond_bq, L1_cond_Wk, L1_cond_bk, L1_cond_Wv, L1_cond_bv, L1_cond_Wo, L1_cond_bo, L1_cond_W1, L1_cond_b1, L1_cond_W2, L1_cond_b2, L1_cond_g2, L1_cond_beta2)
    x = _L2_cond_ref(x, condB_theta, condB_phi)
    x = _L3_cond_ref(x, condB_safetyscore, L3_cond_U, L3_cond_V, L3_cond_safety_bias, L3_cond_gate_w1, L3_cond_gate_b1, L3_cond_gate_w2, L3_cond_gate_b2, L3_cond_resp_w, L3_cond_resp_b)
    return x

_drawn_inputs = setup_inputs


def setup_inputs(seed=0):
    import zlib

    import numpy as np

    out = dict(_drawn_inputs(seed))
    spreads = {'L0_cond_ln_gamma': (1.0, 0.2),
     'L0_cond_ln_beta': (0.0, 0.1),
     'L1_cond_b_ada': (0.0, 0.1),
     'L1_cond_bq': (0.0, 0.8),
     'L1_cond_bk': (0.0, 2.0),
     'L1_cond_bv': (0.0, 0.1),
     'L1_cond_bo': (0.0, 0.1),
     'L1_cond_b1': (0.0, 0.1),
     'L1_cond_b2': (0.0, 0.1),
     'L1_cond_g2': (1.0, 0.2),
     'L1_cond_beta2': (0.0, 0.342),
     'L3_cond_safety_bias': (0.0, 0.352),
     'L3_cond_gate_b1': (0.0, 2.0),
     'L3_cond_resp_b': (0.0, 0.352)}
    factors = {'fside_Bx16xSxS_0': 8.0,
     'L0_cond_down_b': 8.0,
     'L1_cond_Wq': 8.0,
     'L1_cond_Wk': 8.0,
     'L3_cond_V': 64.0,
     'L3_cond_gate_w1': 54.688,
     'L3_cond_gate_w2': 42.992}
    for name, (base, spread) in spreads.items():
        noise = np.random.default_rng([zlib.crc32(name.encode()), seed]).standard_normal(out[name].shape)
        drawn = base * np.exp(spread * noise) if base else spread * noise
        out[name] = jnp.asarray(drawn.astype(out[name].dtype))
    for name, factor in factors.items():
        out[name] = (out[name] * factor).astype(out[name].dtype)
    return out
```

```python
import math
from contextlib import ExitStack

import numpy as np

import concourse.bass as bass
from concourse import mybir

F32 = mybir.dt.float32
F32R = mybir.dt.float32r
BF16 = mybir.dt.bfloat16
I32 = mybir.dt.int32
U8 = mybir.dt.uint8
ALU = mybir.AluOpType
ACT = mybir.ActivationFunctionType
AX = mybir.AxisListType

P = 128
D = 512
DC = D // P
HEADS = 16
HD = D // HEADS
FF = 2048
FC = FF // P
ADAPT = 128
EXPERTS = 16
RANK = 32
TOK = 512
TJ = TOK // P
LN_EPS = 1e-5
GS_EPS = 1e-8
MASKED = -1.0e38
MAX_FLOOR = -3.0e37
C_FREQ, C_IOTA, C_IDENT, C_STACK = 0, 2, 2 + EXPERTS, 2 + EXPERTS + P
C_COLS = C_STACK + HD
TWO_PI_HI, TWO_PI_MID = 6.28125, 0.0019350051879882812
TWO_PI_LO = 2 * math.pi - TWO_PI_HI - TWO_PI_MID
ROUND_MAGIC = 12582912.0
SIN_MAX = 3.1415925


class Parts:
    pass


def after(eng, sem, n):
    if not isinstance(n, int) or n > 0:
        eng.wait_ge(sem, n)


def shape_constants():
    half = D // 2
    freqs = np.exp(np.arange(half, dtype=np.float32) * np.float32(-math.log(10000.0) / (half - 1)))
    out = np.zeros((P, C_COLS), np.float32)
    out[:, C_FREQ:C_FREQ + 2] = freqs.astype(np.float32).reshape(2, P).T
    out[:, C_IOTA:C_IOTA + EXPERTS] = np.arange(EXPERTS, dtype=np.float32)
    out[:, C_IDENT:C_IDENT + P] = np.eye(P, dtype=np.float32)
    out[:, C_STACK:C_STACK + HD] = np.tile(np.eye(HD, dtype=np.float32), (P // HD, 1))
    return out


def rows(ap, n=P):
    return ap.rearrange("(a n) -> a n", a=1).broadcast_to([n, ap.shape[0]])


def rounds(eng, last, batch_of, first_full, last_full, emit):
    n = 0
    while n <= last:
        end = n
        while first_full <= n and end + 1 <= last_full and batch_of(end + 1) == batch_of(n):
            end += 1
        if end > n:
            with eng.Fori(n, end + 1) as i:
                emit(i, n, batch_of(n))
        else:
            emit(n, n, batch_of(n))
        n = end + 1


class Chain:

    def __init__(self, eng, sem, base):
        self.eng, self.sem, self.base, self.n = eng, sem, base, 0

    def __call__(self, ins):
        self.n += 1
        ins.then_inc(self.sem, 1)
        self.eng.wait_ge(self.sem, self.base + self.n)



def setup_stage(nc, net, em):
    B = net.B
    with ExitStack() as ctx:
        def sb(name, shape, dt=F32):
            return ctx.enter_context(nc.sbuf_tensor(name, shape, dt))

        def sem(name):
            return ctx.enter_context(nc.semaphore(name))

        consts = net.consts
        ints = sb("su_ints", [P, 2, B], I32)
        angles_in = sb("su_angles_in", [P, 2, B])
        w_ada = sb("su_w_ada", [P, DC, 2 * D])
        b_ada = sb("su_b_ada", [P, 2 * D])
        experts = sb("su_experts", [P, EXPERTS, P])
        exp_bias = sb("su_exp_bias", [P, EXPERTS])
        exp_emb = sb("su_exp_emb", [P, EXPERTS])
        NA = 4 * B + 4 * B
        ang = sb("su_ang", [P, NA])
        turns = sb("su_turns", [P, NA])
        sins = sb("su_sins", [P, NA])
        idf = sb("su_idf", [P, 2, B])
        idx = sb("su_idx", [P, B])
        valid = sb("su_valid", [P, 2, B])
        hot = sb("su_hot", [P, B, EXPERTS])
        hotv = sb("su_hotv", [P, B, EXPERTS])
        pick = sb("su_pick", [P, EXPERTS])
        bias2 = sb("su_bias2", [P, 2])
        wacc = sb("su_wacc", [P, P])
        sig = sb("su_sig", [P, 4 * B])
        rep = sb("su_rep", [P, 4, B, P])

        ps_ada = [ctx.enter_context(nc.psum_tensor(f"su_ps_ada{i}", [P, 512], F32)) for i in range(2)]

        s_small = sem("su_small_in")
        s_big = sem("su_big_in")
        s_dve = sem("su_dve")
        s_ang = sem("su_angles_ready")
        s_sin = sem("su_sines_ready")
        s_sig = sem("su_sigmoid_ready")
        s_rep = sem("su_columns_ready")
        s_ada = sem("su_ada_done")
        s_ada_out = sem("su_ada_taken")

        block = ctx.enter_context(nc.Block())

        @block.sync
        def _(sp):
            sp.dma_start(consts[:], net.given["shape_consts"]).then_inc(s_small, 16)
            sp.dma_start(ints[:, 0, :], rows(net.given["t_step"])).then_inc(s_small, 16)
            sp.dma_start(ints[:, 1, :], rows(net.given["domain"])).then_inc(s_small, 16)
            sp.dma_start(angles_in[:, 0, :], rows(net.given["theta"])).then_inc(s_small, 16)
            sp.dma_start(angles_in[:, 1, :], rows(net.given["phi"])).then_inc(s_small, 16)
            sp.dma_start(w_ada[:], net.given["W_ada"].rearrange("(c p) n -> p c n", p=P)).then_inc(s_big, 16)
            sp.dma_start(b_ada[:], rows(net.given["b_ada"])).then_inc(s_big, 16)
            sp.dma_start(experts[:], net.given["expert_WT"].rearrange("e a o -> a e o")).then_inc(s_big, 16)
            sp.dma_start(exp_bias[:], net.given["expert_bT"]).then_inc(s_big, 16)
            sp.dma_start(exp_emb[:], net.given["domain_embT"]).then_inc(s_big, 16)
            load_embed_weights(sp, net, em)

        @block.scalar
        def _(act):
            act.wait_ge(s_ang, 1)
            act.activation(sins[:], ang[:], ACT.Sin).then_inc(s_sin, 1)
            act.wait_ge(s_sin, 1)
            act.activation(sig[:], sins[:, 0:4 * B], ACT.Sigmoid).then_inc(s_sig, 1)

        @block.vector
        def _(dve):
            v = nc.vector
            link = Chain(dve, s_dve, 0)
            dve.wait_ge(s_small, 5 * 16)
            ident = consts[:, C_IDENT:C_IDENT + P]
            link(v.tensor_copy(net.ident_bf[:], ident))
            link(v.tensor_copy(idf[:], ints[:]))
            link(v.tensor_scalar(idf[:, 0, :], idf[:, 0, :], 1.0 / 100.0, 4000.0, ALU.mult, ALU.mult))
            for c in range(4):
                f = consts[:, C_FREQ + c % 2:C_FREQ + c % 2 + 1]
                link(v.tensor_scalar(ang[:, c * B:(c + 1) * B], idf[:, 0, :], f, None, ALU.mult))
            for k in range(2):
                for q in range(2):
                    o = 4 * B + (2 * k + q) * B
                    link(v.tensor_copy(ang[:, o:o + B], angles_in[:, k, :]))
            quarter = [(2 * B, 4 * B), (5 * B, 6 * B), (7 * B, 8 * B)]
            sine = [(0, 2 * B), (4 * B, 5 * B), (6 * B, 7 * B)]
            for spans, add in ((sine, 0.0), (quarter, 0.25)):
                for a, b in spans:
                    link(v.tensor_scalar(turns[:, a:b], ang[:, a:b], 1.0 / (2 * math.pi), add, ALU.mult, ALU.add))
            link(v.tensor_scalar(turns[:], turns[:], ROUND_MAGIC, None, ALU.add))
            link(v.tensor_scalar(turns[:], turns[:], ROUND_MAGIC, None, ALU.subtract))
            for part in (TWO_PI_HI, TWO_PI_MID, TWO_PI_LO):
                link(v.scalar_tensor_tensor(ang[:], turns[:], -part, ang[:], ALU.mult, ALU.add))
            for a, b in quarter:
                link(v.tensor_scalar(ang[:, a:b], ang[:, a:b], math.pi / 2, None, ALU.add))
            v.tensor_scalar(ang[:], ang[:], SIN_MAX, -SIN_MAX, ALU.min, ALU.max).then_inc(s_ang, 1)
            dve.wait_ge(s_sig, 1)
            link(v.tensor_tensor(sig[:], sig[:], sins[:, 0:4 * B], ALU.mult))
            for c in range(4):
                for b in range(B):
                    col = sig[:, c * B + b:c * B + b + 1]
                    last = v.tensor_copy(rep[:, c, b, :], col.to_broadcast([P, P]))
            last.then_inc(s_rep, 1)
            for b in range(B):
                for k in range(2):
                    st = sins[:, 4 * B + 2 * k * B + b:4 * B + 2 * k * B + b + 1]
                    ct = sins[:, 5 * B + 2 * k * B + b:5 * B + 2 * k * B + b + 1]
                    cv = net.rot_c[:, b, :].rearrange("p (n f) -> p n f", f=4)
                    sv = net.rot_s[:, b, :].rearrange("p (n f) -> p n f", f=4)
                    for q in range(2):
                        v.tensor_copy(cv[:, :, 2 * k + q], ct.to_broadcast([P, P]))
                    v.tensor_copy(sv[:, :, 2 * k], st.to_broadcast([P, P]))
                    link(v.tensor_scalar(sv[:, :, 2 * k + 1], st.to_broadcast([P, P]), -1.0, None, ALU.mult))

            dve.wait_ge(s_big, 5 * 16)
            dom = idf[:, 1, :]
            link(v.tensor_scalar(idx[:], dom, 0.0, float(EXPERTS - 1), ALU.max, ALU.min))
            link(v.tensor_tensor(valid[:, 0, :], idx[:], dom, ALU.is_equal))
            link(v.tensor_scalar(valid[:, 1, :], valid[:, 0, :], -1.0, 1.0, ALU.mult, ALU.add))
            iota = consts[:, C_IOTA:C_IOTA + EXPERTS]
            for b in range(B):
                link(v.tensor_scalar(hot[:, b, :], iota, idx[:, b:b + 1], None, ALU.is_equal))
                link(v.tensor_scalar(hotv[:, b, :], hot[:, b, :], valid[:, 0, b:b + 1], None, ALU.mult))
                for k, (table, picked) in enumerate(((exp_bias, hotv), (exp_emb, hot))):
                    link(v.tensor_tensor(pick[:], table[:], picked[:, b, :], ALU.mult))
                    link(v.tensor_reduce(bias2[:, k:k + 1], pick[:], AX.X, ALU.add))
                link(v.tensor_tensor(net.exp_bias[:, b:b + 1], bias2[:, 0:1], bias2[:, 1:2], ALU.add))
                link(v.tensor_scalar(wacc[:], ident, valid[:, 1, b:b + 1], None, ALU.mult))
                for e in range(EXPERTS):
                    to = net.exp_w[:, b, :] if e == EXPERTS - 1 else wacc[:]
                    link(v.scalar_tensor_tensor(to, experts[:, e, :], hotv[:, b, e:e + 1], wacc[:], ALU.mult, ALU.add))

            for n in range(2 * B):
                b, k = divmod(n, 2)
                dve.wait_ge(s_ada, n + 1)
                to = net.ada_scale[:, b, :] if k == 0 else net.ada_shift[:, b, :]
                ins = v.tensor_tensor(to, ps_ada[n % 2][:], b_ada[:, k * D:(k + 1) * D], ALU.add)
                ins.then_inc(s_ada_out, 1)
                if k == 0:
                    dve.wait_ge(s_ada_out, n + 1)
                    link(v.tensor_scalar(to, to, 1.0, None, ALU.add))

        @block.tensor
        def _(pe):
            pe.wait_ge(s_rep, 1)
            pe.wait_ge(s_big, 5 * 16)
            for n in range(2 * B):
                b, k = divmod(n, 2)
                after(pe, s_ada_out, n - 1)
                for c in range(DC):
                    last = pe.matmul(ps_ada[n % 2][:], rep[:, c, b, :], w_ada[:, c, k * D:(k + 1) * D],
                                     start=(c == 0), stop=(c == DC - 1))
                last.then_inc(s_ada, 1)



def embed_weights(nc, ctx):
    def sb(name, shape, dt=F32):
        return ctx.enter_context(nc.sbuf_tensor(name, shape, dt))

    em = Parts()
    em.down = sb("em_down", [P, DC, ADAPT])
    em.up = sb("em_up", [ADAPT, D])
    em.wq = sb("em_wq", [P, DC, D])
    em.wk = sb("em_wk", [P, DC, D])
    em.wv = sb("em_wv", [P, DC, D])
    em.down_b = sb("em_down_b", [P, 1])
    em.bqk = sb("em_bqk", [P, 2, DC])
    em.up_b = sb("em_up_b", [P, D])
    em.gamma = sb("em_gamma", [P, D])
    em.beta = sb("em_beta", [P, D])
    em.bv = sb("em_bv", [P, D])
    em.x_in = sb("em_x_in", [P, TJ, D])
    em.gs = [sb(f"em_gs{i}", [P, 2, DC, RANK + 1]) for i in range(2)]
    em.s_x = ctx.enter_context(nc.semaphore("em_x_in_done"))
    em.s_w = ctx.enter_context(nc.semaphore("em_weights_in"))
    em.n_w = 14
    return em


def load_embed_weights(sp, net, em):
    xv = net.given["x"].rearrange("b (t j p) d -> (b t) p j d", j=TJ, p=P)
    sp.dma_start(em.x_in[:], xv[0]).then_inc(em.s_x, 16)
    sp.dma_start(em.down[:], net.given["down_WT"].rearrange("(c p) a -> p c a", p=P)).then_inc(em.s_w, 16)
    sp.dma_start(em.down_b[:], net.given["down_b"].rearrange("(p a) -> p a", a=1)).then_inc(em.s_w, 16)
    sp.dma_start(em.up[:], net.given["up_WT"]).then_inc(em.s_w, 16)
    for to, v in ((em.up_b, net.given["up_b"]), (em.gamma, net.given["ln_gamma"]), (em.beta, net.given["ln_beta"]), (em.bv, net.given["bv"])):
        sp.dma_start(to[:], rows(v)).then_inc(em.s_w, 16)
    for m, w in enumerate((net.given["U"], net.given["V"])):
        sp.dma_start(em.gs[0][:, m, :, 0:RANK], w.rearrange("(c p) r -> p c r", p=P)).then_inc(em.s_w, 16)
    for to, w in ((em.wq, net.given["Wq"]), (em.wk, net.given["Wk"]), (em.wv, net.given["Wv"])):
        sp.dma_start(to[:], w.rearrange("(c p) n -> p c n", p=P)).then_inc(em.s_w, 16)
    for k, v in enumerate((net.given["bq"], net.given["bk"])):
        sp.dma_start(em.bqk[:, k, :], v).then_inc(em.s_w, 16)


def embed_stage(nc, net, em):
    B, S = net.B, net.S
    NB = S // TOK
    NT = B * NB
    with ExitStack() as ctx:
        def sb(name, shape, dt=F32):
            return ctx.enter_context(nc.sbuf_tensor(name, shape, dt))

        def sem(name):
            return ctx.enter_context(nc.semaphore(name))

        minus_half = sb("em_minus_half", [P, TJ])
        eps = sb("em_eps", [P, TJ])
        down, up, wq, wk, wv = em.down, em.up, em.wq, em.wk, em.wv
        down_b, bqk, up_b, gamma, beta, bv = em.down_b, em.bqk, em.up_b, em.gamma, em.beta, em.bv
        x_in, gs, s_x, s_w, n_w = em.x_in, em.gs, em.s_x, em.s_w, em.n_w
        x_up = sb("em_x_up", [P, TJ, D])
        x_t = sb("em_x_t", [P, DC, TOK])
        hid = sb("em_hid", [P, TOK])
        hid2 = sb("em_hid2", [P, TOK])
        res = sb("em_res", [P, TJ, D])
        x1_t = sb("em_x1_t", [P, DC, TOK])
        qk32 = sb("em_qk32", [P, 2, TOK])
        qk_hi = sb("em_qk_hi", [P, 2, DC, TOK], F32R)
        qk_lo = sb("em_qk_lo", [P, 2, DC, TOK], F32R)
        v_out = sb("em_v_out", [P, TJ, D])
        stats = sb("em_stats", [P, TJ, 6])
        mv = sb("em_mv", [P, TJ, 2])
        wait_cell = sb("em_wait_cell", [P, 1])
        rstd = sb("em_rstd", [P, TJ])
        gs_row = sb("em_gs_columns", [P, 2, DC, P])
        gs_norm = sb("em_gs_norms", [P, 4])
        half_of = sb("em_half", [P, 2])
        gs_eps = sb("em_gs_eps", [P, 2])
        gs_coef = sb("em_gs_coef", [P, 2, RANK])
        gs_proj = sb("em_gs_proj", [P, 2, DC, RANK])
        gs_col = sb("em_gs_unit", [P, 2, DC])
        gsq = sb("em_gs_basis", [P, 2, DC, RANK])
        vtv = sb("em_vtv", [RANK, RANK])
        u_top = sb("em_u_top", [RANK, RANK])
        u_t = sb("em_u_t", [RANK, D])
        mid = sb("em_mid", [RANK, RANK])

        ps_t = [ctx.enter_context(nc.psum_tensor(f"em_ps_t{i}", [P, 512], F32)) for i in range(4)]
        ps_m = [ctx.enter_context(nc.psum_tensor(f"em_ps_m{i}", [P, 512], F32)) for i in range(4)]

        s_xt = sem("em_x_transposed")
        s_xt_out = sem("em_x_t_ready")
        s_x1t = sem("em_x1_transposed")
        s_x1t_out = sem("em_x1_t_ready")
        s_down = sem("em_down_done")
        s_gelu = sem("em_gelu_ready")
        s_exp = sem("em_expert_done")
        s_hid2 = sem("em_expert_ready")
        s_up = sem("em_up_done")
        s_res = sem("em_res_ready")
        s_q = sem("em_qk_done")
        s_qk32 = sem("em_qk_taken")
        s_split = sem("em_qk_split")
        s_v = sem("em_v_done")
        s_v_out = sem("em_v_ready")
        s_xup = sem("em_x_up_ready")
        s_mv = sem("em_moments")
        s_rs = sem("em_rstd_ready")
        s_n1 = sem("em_norm_scaled")
        s_x0 = sem("em_affine_ready")
        s_link = sem("em_dve_steps")
        s_plink = sem("em_pool_steps")
        s_split_link = sem("em_split_steps")
        s_x1_st = sem("em_x1_stored")
        s_qk_st = [sem(f"em_{a}_stored") for a in "qk"]
        s_v_st = sem("em_v_stored")
        s_gsr = sem("em_gs_columns_ready")
        s_dot = sem("em_gs_dots")
        s_n2 = sem("em_gs_squares")
        s_nrm = sem("em_gs_norms_ready")
        s_gs = sem("em_gs_dve_steps")
        s_gpool = sem("em_gs_pool_steps")
        s_end = sem("em_end_done")
        s_end_out = sem("em_end_taken")
        per_round = RANK // NT
        per_turn = per_round // 4

        def batch_of(n):
            return min(n, NT - 1) // NB

        def drive(eng, emit):
            rounds(eng, NT, batch_of, 2, NT - 2, emit)

        block = ctx.enter_context(nc.Block())

        @block.sync
        def _(sp):
            xv = net.given["x"].rearrange("b (t j p) d -> (b t) p j d", j=TJ, p=P)
            x1v = net.x1.rearrange("(t j p) d -> t p j d", j=TJ, p=P)
            vv = net.v.rearrange("(t j p) d -> t p j d", j=TJ, p=P)

            def emit(n, n0, b):
                p = n - 1
                if n0 < NT - 1:
                    sp.wait_ge(s_xup, n + 1)
                    sp.wait_ge(s_xt, 4 * n + 4)
                    sp.dma_start(x_in[:], xv[n + 1]).then_inc(s_x, 16)
                if n0 >= 1:
                    sp.wait_ge(s_x0, 8 * p + 8)
                    sp.dma_start(x1v[p], res[:]).then_inc(s_x1_st, 16)
                    for k, (hi, lo) in enumerate(((net.q_hi, net.q_lo), (net.k_hi, net.k_lo))):
                        sp.wait_ge(s_split, 8 * p + 4 * k + 4)
                        for to, frm in ((hi, qk_hi), (lo, qk_lo)):
                            tv = to.rearrange("(c p) (t n) -> t p c n", p=P, n=TOK)
                            sp.dma_start(tv[p], frm[:, k].bitcast(F32)).then_inc(s_qk_st[k], 16)
                    sp.wait_ge(s_v_out, 4 * p + 4)
                    sp.dma_start(vv[p], v_out[:]).then_inc(s_v_st, 16)

            drive(sp, emit)
            sp.wait_ge(s_x1_st, 16 * NT)
            sp.wait_ge(s_qk_st[0], 32 * NT)
            sp.wait_ge(s_qk_st[1], 32 * NT)
            sp.wait_ge(s_v_st, 16 * NT)

        @block.tensor
        def _(pe):
            ident = net.consts[:, C_IDENT:C_IDENT + P]
            pe.wait_ge(s_w, 16 * n_w)

            def emit(n, n0, b):
                p = n - 1

                def gs_dots(turn):
                    for k in range(turn * per_turn, (turn + 1) * per_turn):
                        pe.wait_ge(s_gsr, p * per_round + k + 1)
                        for m in range(2):
                            for c in range(DC):
                                last = pe.matmul(ps_t[0][:, m * (RANK + 1):(m + 1) * (RANK + 1)], gs_row[:, m, c, :],
                                                 gs[k % 2][:, m, c, :], start=(c == 0), stop=(c == DC - 1))
                        last.then_inc(s_dot, 1)

                if n0 >= 2:
                    pe.wait_ge(s_gsr, p * per_round + 1)
                if n0 >= 1:
                    for c in range(DC):
                        pe.wait_ge(s_x0, 8 * p + 8)
                        pe.wait_ge(s_xt_out, 4 * p + c + 1)
                        for j in range(TJ):
                            last = pe.transpose(ps_t[c][:, j * P:(j + 1) * P], res[:, j, c * P:(c + 1) * P], ident)
                        last.then_inc(s_x1t, 1)
                if n0 < NT:
                    pe.wait_ge(s_x, 16 * (n + 1))
                    for c in range(DC):
                        if n0 >= 1:
                            pe.wait_ge(s_x1t_out, 4 * p + c + 1)
                        for j in range(TJ):
                            last = pe.transpose(ps_t[c][:, j * P:(j + 1) * P], x_in[:, j, c * P:(c + 1) * P], ident)
                        last.then_inc(s_xt, 1)
                    if n0 >= 2:
                        pe.wait_ge(s_v_out, 4 * (n - 2) + 4)
                    for c in range(DC):
                        pe.wait_ge(s_xt_out, 4 * n + c + 1)
                        last = pe.matmul(ps_m[0][:], down[:, c, :], x_t[:, c, :], start=(c == 0), stop=(c == DC - 1))
                    last.then_inc(s_down, 1)
                    pe.wait_ge(s_gelu, n + 1)
                    pe.matmul(ps_m[1][:], net.exp_w[:, b, :], hid[:], start=True, stop=True).then_inc(s_exp, 1)
                    pe.wait_ge(s_hid2, n + 1)
                    for j in range(TJ):
                        pe.matmul(ps_m[j][:], hid2[:, j * P:(j + 1) * P], up[:], start=True, stop=True).then_inc(s_up, 1)
                if n0 >= 1:
                    if n0 == NT:
                        pe.wait_ge(s_x1t_out, 4 * p + 1)
                    for c in range(DC):
                        if c == 0:
                            gs_dots(0)
                        if n0 < NT:
                            pe.wait_ge(s_res, 4 * n + c + 1)
                        else:
                            after(pe, s_v_out, 4 * (p - 1) + c + 1)
                        for k in range(DC):
                            pe.wait_ge(s_x1t_out, 4 * p + k + 1)
                            last = pe.matmul(ps_m[c][:], wq[:, k, c * P:(c + 1) * P], x1_t[:, k, :],
                                             start=(k == 0), stop=(k == DC - 1))
                        last.then_inc(s_q, 1)
                    for c in range(DC):
                        if c in (0, 2):
                            gs_dots(1 + c // 2)
                        pe.wait_ge(s_qk32, 8 * p + c + 1)
                        for k in range(DC):
                            last = pe.matmul(ps_m[c][:], wk[:, k, c * P:(c + 1) * P], x1_t[:, k, :],
                                             start=(k == 0), stop=(k == DC - 1))
                        last.then_inc(s_q, 1)
                    for j in range(TJ):
                        if j == 0:
                            gs_dots(3)
                        pe.wait_ge(s_qk32, 8 * p + 4 + j + 1)
                        for k in range(DC):
                            last = pe.matmul(ps_m[j][:], x1_t[:, k, j * P:(j + 1) * P], wv[:, k, :],
                                             start=(k == 0), stop=(k == DC - 1))
                        last.then_inc(s_v, 1)

            drive(pe, emit)

            pe.wait_ge(s_gsr, RANK + 1)
            for c in range(DC):
                last = pe.matmul(ps_t[0][0:RANK, 0:RANK], gsq[:, 1, c, :], gsq[:, 1, c, :],
                                 start=(c == 0), stop=(c == DC - 1))
            last.then_inc(s_end, 1)
            for c in range(DC):
                last = pe.transpose(ps_t[1][0:RANK, c * P:(c + 1) * P], gsq[:, 0, c, :], ident)
            last.then_inc(s_end, 1)
            pe.wait_ge(s_end_out, 1)
            pe.transpose(ps_t[0][0:RANK, 0:RANK], gsq[0:RANK, 0, 0, :], ident[0:RANK, 0:RANK]).then_inc(s_end, 1)
            pe.wait_ge(s_end_out, 3)
            pe.matmul(ps_t[1][0:RANK, 0:RANK], vtv[:], u_top[:], start=True, stop=True).then_inc(s_end, 1)
            pe.wait_ge(s_end_out, 4)
            for c in range(DC):
                last = pe.matmul(ps_t[0][:, c * RANK:(c + 1) * RANK], u_t[:, c * P:(c + 1) * P], mid[:],
                                 start=True, stop=True)
            last.then_inc(s_end, 1)

        @block.scalar
        def _(act):
            act.wait_ge(s_w, 16 * n_w)

            def emit(n, n0, b):
                p = n - 1
                if n0 >= 1:
                    for c in range(DC):
                        act.wait_ge(s_x1t, 4 * p + c + 1)
                        if n0 >= 2:
                            act.wait_ge(s_v, 4 * p)
                        act.activation(x1_t[:, c, :], ps_t[c][:], ACT.Copy).then_inc(s_x1t_out, 1)
                if n0 < NT:
                    for c in range(DC):
                        act.wait_ge(s_xt, 4 * n + c + 1)
                        if n0 >= 1:
                            act.wait_ge(s_down, n)
                        act.activation(x_t[:, c, :], ps_t[c][:], ACT.Copy).then_inc(s_xt_out, 1)
                    act.wait_ge(s_down, n + 1)
                    if n0 >= 1:
                        act.wait_ge(s_exp, n)
                    act.activation(hid[:], ps_m[0][:], ACT.Gelu, bias=down_b[:, 0:1]).then_inc(s_gelu, 1)
                if n0 >= 1:
                    for k in range(2):
                        for c in range(DC):
                            g = 4 * k + c
                            act.wait_ge(s_q, 8 * p + g + 1)
                            if n0 >= 2 or g >= 2:
                                act.wait_ge(s_split, 8 * p + g - 1)
                            act.activation(qk32[:, g % 2, :], ps_m[c][:], ACT.Identity,
                                           bias=bqk[:, k, c:c + 1]).then_inc(s_qk32, 1)

            drive(act, emit)

        @block.gpsimd
        def _(pool):
            step = Chain(pool, s_plink, 0)
            step(pool.memset(minus_half[:], -0.5))
            step(pool.memset(eps[:], LN_EPS))
            step(pool.memset(half_of[:], 0.5))
            step(pool.memset(gs_eps[:], GS_EPS))
            pool.wait_ge(s_w, 16 * n_w)

            def emit(n, n0, b):
                def gs_norms(turn):
                    if n0 < 1:
                        return
                    for k in range(turn * per_turn, (turn + 1) * per_turn):
                        i = (n - 1) * per_round + k
                        pool.wait_ge(s_n2, i + 1)
                        glink = Chain(pool, s_gpool, i)
                        glink(pool.tensor_tensor(gs_norm[:, 2:4], gs_norm[:, 0:2], half_of[:], ALU.pow))
                        pool.tensor_tensor(gs_norm[:, 2:4], gs_norm[:, 2:4], gs_eps[:], ALU.add).then_inc(s_nrm, 1)

                if n0 >= NT:
                    for turn in range(4):
                        gs_norms(turn)
                    return
                link = Chain(pool, s_plink, n * 2 + 4)
                pool.wait_ge(s_x, 16 * (n + 1))
                if n0 >= 1:
                    pool.wait_ge(s_res, 4 * n)
                pool.tensor_tensor(x_up[:], x_in[:], up_b[:].unsqueeze(1).broadcast_to([P, TJ, D]),
                                   ALU.add).then_inc(s_xup, 1)
                for half in range(2):
                    pool.wait_ge(s_mv, 2 * n + half + 1)
                    link(pool.tensor_tensor(rstd[:], mv[:, :, 1], eps[:], ALU.add))
                    pool.tensor_tensor(rstd[:], rstd[:], minus_half[:], ALU.pow).then_inc(s_rs, 1)
                    gs_norms(2 * half)
                    for j in range(TJ):
                        pool.wait_ge(s_n1, 8 * n + 4 * half + j + 1)
                        if half == 0:
                            pool.tensor_tensor(res[:, j, :], res[:, j, :], beta[:], ALU.add).then_inc(s_x0, 1)
                        else:
                            pool.tensor_tensor(res[:, j, :], res[:, j, :], net.ada_shift[:, b, :],
                                               ALU.add).then_inc(s_x0, 1)
                    gs_norms(2 * half + 1)

            drive(pool, emit)

        @block.vector
        def _(dve):
            v = nc.vector
            dve.wait_ge(s_w, 16 * n_w)

            def gs_columns(src):
                v.tensor_copy(gs_row[:], src[:, :, :, 0:1].broadcast_to([P, 2, DC, P])).then_inc(s_gsr, 1)

            for m in range(2):
                last = v.memset(gs[m][:, :, :, RANK:RANK + 1], 0.0)
            last.then_inc(s_gs, 1)
            gs_columns(gs[0])

            def emit(n, n0, b):
                p = n - 1
                link = Chain(dve, s_link, n * 2 * (TJ + 1))

                def gs_turn(turn):
                    if n0 < 1:
                        return
                    for k in range(turn * per_turn, (turn + 1) * per_turn):
                        i = p * per_round + k
                        src, to = gs[k % 2], gs[(k + 1) % 2]
                        dots = ps_t[0][:, 0:2 * (RANK + 1)].rearrange("p (m r) -> p m r", m=2)
                        step = Chain(dve, s_gs, i * 5 + 1)
                        dve.wait_ge(s_dot, i + 1)
                        v.tensor_copy(gs_norm[:, 0:2].unsqueeze(2), dots[:, :, 0:1]).then_inc(s_n2, 1)
                        dve.wait_ge(s_nrm, i + 1)
                        step(v.reciprocal(gs_norm[:, 2:4], gs_norm[:, 2:4]))
                        over = gs_norm[:, 2:4].unsqueeze(2)
                        v.tensor_tensor(gs_coef[:], dots[:, :, 1:RANK + 1], over.broadcast_to([P, 2, RANK]), ALU.mult)
                        step(v.tensor_tensor(gs_col[:], src[:, :, :, 0], over.broadcast_to([P, 2, DC]), ALU.mult))
                        step(v.tensor_copy(gsq[:, :, :, bass.ds(i, 1)], gs_col[:].unsqueeze(3)))
                        step(v.tensor_tensor(gs_proj[:], gs_col[:].unsqueeze(3).broadcast_to([P, 2, DC, RANK]),
                                             gs_coef[:].unsqueeze(2).broadcast_to([P, 2, DC, RANK]), ALU.mult))
                        step(v.tensor_tensor(to[:, :, :, 0:RANK], src[:, :, :, 1:RANK + 1], gs_proj[:], ALU.subtract))
                        gs_columns(to)
                unscale = 1.0 / math.sqrt(HD)
                slink = Chain(dve, s_split_link, p * 2 * DC)

                def splits(g0):
                    if n0 < 1:
                        return
                    for g in (g0, g0 + 1):
                        k, c = divmod(g, 4)
                        dve.wait_ge(s_qk32, 8 * p + g + 1)
                        if n0 >= 2 and g0 % 4 == 0:
                            dve.wait_ge(s_qk_st[k], 32 * p)
                        frm = qk32[:, g % 2, :]
                        factor = unscale if k == 0 else 1.0
                        slink(v.tensor_scalar(qk_hi[:, k, c, :], frm, factor, None, ALU.mult))
                        v.scalar_tensor_tensor(qk_lo[:, k, c, :], frm, factor, qk_hi[:, k, c, :].bitcast(F32),
                                               ALU.mult, ALU.subtract).then_inc(s_split, 1)

                def moments(half):
                    for j in range(TJ):
                        if half == 1:
                            dve.wait_ge(s_x0, 8 * n + j + 1)
                        last = v.bn_stats(stats[:, j, :], res[:, j, :])
                    link(last)
                    v.memset(wait_cell[:], 0.0)
                    for j in range(TJ):
                        last = v.bn_aggr(mv[:, j, :], stats[:, j, :])
                    last.then_inc(s_mv, 1)

                def scaled(half):
                    factor = gamma[:] if half == 0 else net.ada_scale[:, b, :]
                    dve.wait_ge(s_rs, 2 * n + half + 1)
                    for j in range(TJ):
                        link(v.tensor_scalar(res[:, j, :], res[:, j, :], mv[:, j, 0:1], rstd[:, j:j + 1],
                                             ALU.subtract, ALU.mult))
                        v.tensor_tensor(res[:, j, :], res[:, j, :], factor, ALU.mult).then_inc(s_n1, 1)

                if n0 < NT:
                    dve.wait_ge(s_exp, n + 1)
                    if n0 >= 1:
                        dve.wait_ge(s_up, 4 * n)
                    v.tensor_scalar(hid2[:], ps_m[1][:], net.exp_bias[:, b:b + 1], None, ALU.add).then_inc(s_hid2, 1)
                    dve.wait_ge(s_xup, n + 1)
                    for j in range(TJ):
                        dve.wait_ge(s_up, 4 * n + j + 1)
                        if n0 >= 1 and j == 0:
                            dve.wait_ge(s_x1t, 4 * p + 4)
                            dve.wait_ge(s_x1_st, 16 * p + 16)
                        v.tensor_tensor(res[:, j, :], ps_m[j][:], x_up[:, j, :], ALU.add).then_inc(s_res, 1)
                    dve.wait_ge(s_res, 4 * n + 4)
                    moments(0)
                gs_turn(0)
                splits(0)
                if n0 < NT:
                    scaled(0)
                splits(2)
                gs_turn(1)
                if n0 < NT:
                    moments(1)
                splits(4)
                gs_turn(2)
                if n0 < NT:
                    scaled(1)
                splits(6)
                gs_turn(3)
                if n0 >= 1:
                    for j in range(TJ):
                        dve.wait_ge(s_v, 4 * p + j + 1)
                        if n0 >= 2 and j == 0:
                            dve.wait_ge(s_v_st, 16 * p)
                        v.tensor_tensor(v_out[:, j, :], ps_m[j][:], bv[:], ALU.add).then_inc(s_v_out, 1)

            drive(dve, emit)

            ends = [(vtv[:], ps_t[0][0:RANK, 0:RANK]), (u_t[:], ps_t[1][0:RANK, :]),
                    (u_top[:], ps_t[0][0:RANK, 0:RANK]), (mid[:], ps_t[1][0:RANK, 0:RANK]),
                    (net.basis[:].rearrange("p c r -> p (c r)"), ps_t[0][:, 0:DC * RANK])]
            for n, (to, frm) in enumerate(ends):
                dve.wait_ge(s_end, n + 1)
                v.tensor_copy(to, frm).then_inc(s_end_out, 1)



def attention_stage(nc, net):
    B, S = net.B, net.S
    QB = S // P
    KC = S // 512
    HC = KC // 2
    HALF = S // 2
    GH = 4
    G = HEADS // GH
    RING = 8
    PCOLS = S - 512
    LOOPS = QB // 2
    with ExitStack() as ctx:
        def sb(name, shape, dt=F32):
            return ctx.enter_context(nc.sbuf_tensor(name, shape, dt))

        def sem(name):
            return ctx.enter_context(nc.semaphore(name))

        tiles = sb("at_tiles", [P, RING, S])
        k_st = [sb(f"at_k_stack{i}", [P, GH, S], F32R) for i in range(2)]
        v_sb = [sb(f"at_v{i}", [P, QB, GH * HD]) for i in range(2)]
        q_st = [sb(f"at_q_stack{i}", [P, GH, P], F32R) for i in range(2)]
        mask8 = [sb(f"at_mask8_{i}", [P, S], U8) for i in range(2)]
        negm = [sb(f"at_negmask{i}", [P, S], BF16) for i in range(2)]
        p_t = [sb(f"at_prob_t{i}", [P, S]) for i in range(2)]
        cx_sb = [sb(f"at_ctx_parts{i}", [P, GH * P]) for i in range(2)]
        cx_out = [sb(f"at_ctx_out{i}", [P, GH * HD]) for i in range(2)]
        rmax = sb("at_rmax", [P, RING, 2])
        nmax = sb("at_nmax", [P, RING])
        wait_cell = sb("at_wait_cell", [P, RING, 2])
        rsum = sb("at_rsum", [P, RING, 2])
        rinv = sb("at_rinv", [P, 2, GH])

        ps_s = ctx.enter_context(nc.psum_tensor("at_ps_s", [P, max(KC, 2) * 512], F32))
        ps_p = [ctx.enter_context(nc.psum_tensor(f"at_ps_p{i}", [P, 512], F32)) for i in range(2)]
        ps_c = [ctx.enter_context(nc.psum_tensor(f"at_ps_c{i}", [P, 512], F32)) for i in range(2)]

        s_bias = [sem(f"at_bias_in{i}") for i in range(RING)]
        s_mask = [sem(f"at_mask_in{i}") for i in range(2)]
        s_qin = [sem(f"at_q_in{i}") for i in range(2)]
        s_kin = [sem(f"at_kv_in{i}") for i in range(2)]
        s_nm = sem("at_negmask_ready")
        s_pool = sem("at_bias_masked")
        s_qk = sem("at_qk_done")
        s_sc = sem("at_scores_ready")
        s_max = sem("at_max_ready")
        s_exp = sem("at_exp_ready")
        s_pt = [sem(f"at_probs_transposed{i}") for i in range(2)]
        s_pe = [sem(f"at_probs_t_ready{i}") for i in range(2)]
        s_pv = sem("at_pv_done")
        s_cxs = sem("at_ctx_parts_ready")
        s_cxm = sem("at_ctx_summed")
        s_cxo = sem("at_ctx_ready")
        s_dl = sem("at_dve_steps")
        s_st = [sem(f"at_ctx_stored{i}") for i in range(2)]

        C_NM, C_QK, C_SC, C_PE, C_PV, C_CXM, C_CXO = 2, 16, 2, 1, 2, 2, 2
        C_PT1 = 4 * KC
        C_ST = 16
        def dve_takes(s, c):
            return c % 2 == 1 and (s % 2 == 0 or c == 1)

        def groups(eng, emit):
            with eng.Fori(0, B) as b:
                with eng.Fori(0, G // 2) as gp:
                    for par in range(2):
                        emit(b, gp * 2 + par, par, b * G + gp * 2 + par)

        block = ctx.enter_context(nc.Block())

        @block.sync
        def _(sp):
            bias_v = net.given["bias"].rearrange("b h (t p) k -> (b h t) p k", p=P)
            mask_v = net.given["mask"].rearrange("b o (t p) k -> (b o t) p k", p=P)
            kv = [a.rearrange("(g h d) (b s) -> b g d h s", h=GH, d=HD, s=S) for a in (net.k_hi, net.k_lo)]
            qv = [a.rearrange("(g h d) (b t q) -> b g t d h q", h=GH, d=HD, b=B, q=P) for a in (net.q_hi, net.q_lo)]
            vv = net.v.rearrange("(b t p) (g c) -> b g p t c", b=B, p=P, g=G)

            def load_kv(par, b, g):
                for part in range(4):
                    sp.dma_start(k_st[par][part * HD:(part + 1) * HD].bitcast(F32), kv[part // 2][b, g]).then_inc(s_kin[par], 16)
                sp.dma_start(v_sb[par][:], vv[b, g]).then_inc(s_kin[par], 16)

            load_kv(0, 0, 0)

            def emit(b, g, par, bg, lead=False):
                def pair(it, heads=(GH, GH)):
                    for q2 in range(2):
                        w = bg * QB + it * 2 + q2
                        qb = it * 2 + q2
                        sp.wait_ge(s_qk, 8 * w + 8 - 16 + C_QK)
                        for part in range(4):
                            sp.dma_start(q_st[q2][part * HD:(part + 1) * HD].bitcast(F32),
                                         qv[part % 2][b, g, qb]).then_inc(s_qin[q2], 16)
                        sp.wait_ge(s_nm, w - 1 + C_NM)
                        sp.dma_start(mask8[q2][:], mask_v[b * QB + qb]).then_inc(s_mask[q2], 16)
                        for h in range(heads[q2]):
                            u = w * GH + h
                            r = q2 * GH + h
                            sp.wait_ge(s_pt[1], (u - 7) * HC + C_PT1)
                            sp.dma_start(tiles[:, r, :], bias_v[((0 if lead else bg) * GH + h) * QB + qb]).then_inc(s_bias[r], 16)

                if lead:
                    pair(0, (2, 0))
                    return
                pair(0)
                sp.wait_ge(s_pv, bg * QB * GH + C_PV)
                load_kv(1 - par, (b + (g + 1) // G) % B, (g + 1) % G)
                with sp.Fori(1, LOOPS) as it:
                    pair(it)

            groups(sp, emit)
            emit(0, 0, 0, B * G, lead=True)
            sp.wait_ge(s_kin[0], 80 * (B * G // 2 + 1))
            for q2 in range(2):
                sp.wait_ge(s_qin[q2], 64 * (B * G * LOOPS + 1))
                sp.wait_ge(s_mask[q2], 16 * (B * G * LOOPS + 1))
                sp.wait_ge(s_bias[q2], 16 * (B * G * LOOPS + 1))

        @block.gpsimd
        def _(pool):
            def masked(bg, it, s):
                q2, h = divmod(s, GH)
                w = bg * QB + it * 2 + q2
                pool.wait_ge(s_bias[s], (bg * LOOPS + it) * 16 + 16)
                if h == 0:
                    pool.wait_ge(s_nm, w + 1 + C_NM)
                pool.tensor_tensor(tiles[:, s, 0:PCOLS], tiles[:, s, 0:PCOLS], negm[q2][:, 0:PCOLS],
                                   ALU.add).then_inc(s_pool, 1)

            def emit(b, g, par, bg):
                with pool.Fori(0, LOOPS) as it:
                    for s in range(RING):
                        masked(bg, it, s)

            groups(pool, emit)
            for s in range(2):
                masked(B * G, 0, s)

        @block.tensor
        def _(pe):
            ident = net.consts[:, C_IDENT:C_IDENT + P]
            stack = net.consts[:, C_STACK:C_STACK + HD]
            pe.nop().then_inc(s_qk, C_QK)
            pe.nop().then_inc(s_pt[1], C_PT1)
            pe.nop().then_inc(s_pv, C_PV)
            pe.nop().then_inc(s_cxm, C_CXM)

            def emit(b, g, par, bg, lead=False):
                def qk(it, s, side=par):
                    q2, h = divmod(s, GH)
                    w = bg * QB + it * 2 + q2
                    u = w * GH + h
                    if h == 0:
                        pe.wait_ge(s_qin[q2], (bg * LOOPS + it) * 64 + 64)
                    for a in range(2):
                        pe.wait_ge(s_sc, 2 * (u - 1) + a + 1 + C_SC)
                        for c in range(a * HC, (a + 1) * HC):
                            out = ps_s[:, c * 512:(c + 1) * 512]
                            masked = c == KC - 1
                            last = pe.matmul(out, q_st[q2][:, h, :], k_st[side][:, h, c * 512:(c + 1) * 512],
                                             start=True, stop=not masked)
                            if masked:
                                if h == 0:
                                    pe.wait_ge(s_nm, w + 1 + C_NM)
                                last = pe.matmul(out, net.ident_bf[:], negm[q2][:, PCOLS:S], start=False, stop=True)
                        last.then_inc(s_qk, 1)

                def transposes(it, s, chunks):
                    q2, h = divmod(s, GH)
                    u = (bg * QB + it * 2 + q2) * GH + h
                    for c in chunks:
                        pe.wait_ge(s_exp, 2 * u + c // HC + 1)
                        pe.wait_ge(s_pe[c % 2], u * HC + c // 2 + C_PE)
                        for y in range(4):
                            last = pe.transpose(ps_p[c % 2][:, y * P:(y + 1) * P],
                                                tiles[:, s, (4 * c + y) * P:(4 * c + y + 1) * P], ident)
                        last.then_inc(s_pt[c % 2], 1)

                def pv(it, s, chunks):
                    q2, h = divmod(s, GH)
                    w = bg * QB + it * 2 + q2
                    u = w * GH + h
                    for c in chunks:
                        if h == 0 and c == 0:
                            pe.wait_ge(s_cxo, w - 1 + C_CXO)
                        pe.wait_ge(s_pe[c % 2], u * HC + c // 2 + 1 + C_PE)
                        for y in range(4):
                            t = 4 * c + y
                            last = pe.matmul(ps_c[q2][y * HD:(y + 1) * HD, h * P:(h + 1) * P],
                                             v_sb[par][:, t, h * HD:(h + 1) * HD], p_t[s % 2][:, t * P:(t + 1) * P],
                                             start=(c == 0), stop=(c == KC - 1))
                    if chunks[-1] == KC - 1:
                        last.then_inc(s_pv, 1)

                def parts_sum(it, q2):
                    w = bg * QB + it * 2 + q2
                    pe.wait_ge(s_cxs, w + 1)
                    for h in range(GH):
                        last = pe.matmul(ps_c[q2][:, h * HD:(h + 1) * HD], cx_sb[q2][:, h * P:(h + 1) * P], stack,
                                         start=True, stop=True)
                    last.then_inc(s_cxm, 1)

                def slots(it, first, final):
                    for s in range(RING):
                        if final and s + 2 == RING:
                            pe.wait_ge(s_kin[1 - par], (bg + par) * 40 + 80)
                        qk(it + (s + 2) // RING, (s + 2) % RING, 1 - par if final and s + 2 >= RING else par)
                        if s % GH == 1 and not (first and s < GH):
                            if s < GH:
                                parts_sum(it - 1, 1)
                            else:
                                parts_sum(it, 0)
                        transposes(it, s, range(HC))
                        if s > 0:
                            pv(it, s - 1, range(HC, KC))
                        elif not first:
                            pv(it - 1, RING - 1, range(HC, KC))
                        transposes(it, s, range(HC, KC))
                        pv(it, s, range(HC))
                    if final:
                        pv(it, RING - 1, range(HC, KC))
                        parts_sum(it, 1)

                if lead:
                    pe.wait_ge(s_kin[0], 80)
                    qk(0, 0)
                    qk(0, 1)
                    return
                slots(0, True, False)
                if LOOPS > 2:
                    with pe.Fori(1, LOOPS - 1) as it:
                        slots(it, False, False)
                slots(LOOPS - 1, False, True)

            emit(0, 0, 0, 0, lead=True)
            groups(pe, emit)

        @block.scalar
        def _(act):
            cxv = net.ctx.rearrange("(t p) (g c) -> t g p c", p=P, g=G)

            def emit(b, g, par, bg, lead=False):
                def exp(it, s, a):
                    q2, h = divmod(s, GH)
                    w = bg * QB + it * 2 + q2
                    u = w * GH + h
                    if a == 0:
                        act.wait_ge(s_max, u + 1)
                        if h == 0:
                            act.wait_ge(s_cxo, w - 1 + C_CXO)
                    half = tiles[:, s, a * HALF:(a + 1) * HALF]
                    act.activation(half, half, ACT.Exp, bias=nmax[:, s:s + 1],
                                   accum_out=rsum[:, s, a:a + 1]).then_inc(s_exp, 1)

                def take(it, s, chunks):
                    q2, h = divmod(s, GH)
                    u = (bg * QB + it * 2 + q2) * GH + h
                    for c in chunks:
                        if dve_takes(s, c):
                            continue
                        act.wait_ge(s_pt[c % 2], u * HC + c // 2 + 1 + (C_PT1 if c % 2 else 0))
                        act.wait_ge(s_pv, u - 1 + C_PV)
                        act.activation(p_t[s % 2][:, c * 512:(c + 1) * 512], ps_p[c % 2][:],
                                       ACT.Copy).then_inc(s_pe[c % 2], 1)

                def parts(it, q2):
                    w = bg * QB + it * 2 + q2
                    act.wait_ge(s_pv, GH * w + GH + C_PV)
                    act.wait_ge(s_cxm, w - 1 + C_CXM)
                    act.activation(cx_sb[q2][:], ps_c[q2][:], ACT.Copy).then_inc(s_cxs, 1)

                def store(it, q2):
                    w = bg * QB + it * 2 + q2
                    act.wait_ge(s_cxo, w + 1 + C_CXO)
                    act.dma_start(cxv[b * QB + it * 2 + q2, g], cx_out[q2][:]).then_inc(s_st[q2], 16)

                def slots(it, first, final):
                    for s in range(RING):
                        nxt = (it + (s + 1) // RING, (s + 1) % RING)
                        exp(*nxt, 0)
                        take(it, s, range(HC))
                        if s % GH == 0 and not (first and s < GH):
                            parts(*((it - 1, 1) if s < GH else (it, 0)))
                        exp(*nxt, 1)
                        take(it, s, range(HC, KC))
                        if s % GH == 3 and not (first and s < GH):
                            store(*((it - 1, 1) if s < GH else (it, 0)))
                    if final:
                        parts(it, 1)
                        store(it, 1)

                if lead:
                    exp(0, 0, 0)
                    exp(0, 0, 1)
                    return
                slots(0, True, False)
                if LOOPS > 2:
                    with act.Fori(1, LOOPS - 1) as it:
                        slots(it, False, False)
                slots(LOOPS - 1, False, True)

            emit(0, 0, 0, 0, lead=True)
            groups(act, emit)
            for q2 in range(2):
                act.wait_ge(s_st[q2], 16 * B * G * LOOPS + C_ST)

        @block.vector
        def _(dve):
            v = nc.vector
            v.nop().then_inc(s_nm, C_NM)
            v.nop().then_inc(s_sc, C_SC)
            v.nop().then_inc(s_pe[0], C_PE)
            v.nop().then_inc(s_pe[1], C_PE)
            v.nop().then_inc(s_cxo, C_CXO)
            v.nop().then_inc(s_st[0], C_ST)
            v.nop().then_inc(s_st[1], C_ST)

            def emit(b, g, par, bg, lead=False):
                def convert(it, q2):
                    dve.wait_ge(s_mask[q2], (bg * LOOPS + it) * 16 + 16)
                    v.tensor_scalar(negm[q2][:], mask8[q2][:], MASKED, None, ALU.mult).then_inc(s_nm, 1)

                def scores(it, s, a):
                    q2, h = divmod(s, GH)
                    u = (bg * QB + it * 2 + q2) * GH + h
                    if a == 0:
                        dve.wait_ge(s_pool, u + 1)
                    else:
                        dve.wait_ge(s_sc, 2 * u + 1 + C_SC)
                    dve.wait_ge(s_qk, 2 * u + a + 1 + C_QK)
                    half = tiles[:, s, a * HALF:(a + 1) * HALF]
                    v.memset(wait_cell[:, s, a:a + 1], 0.0)
                    v.tensor_tensor_reduce(out=half, in0=ps_s[:, a * HALF:(a + 1) * HALF], in1=half, scale=1.0,
                                           scalar=MAX_FLOOR if a == 0 else rmax[:, s, 0:1], op0=ALU.add, op1=ALU.max,
                                           accum_out=rmax[:, s, a:a + 1]).then_inc(s_sc, 1)
                    if a == 1:
                        dve.wait_ge(s_sc, 2 * u + 2 + C_SC)
                        v.tensor_scalar(nmax[:, s:s + 1], rmax[:, s, 1:2], -1.0, None, ALU.mult).then_inc(s_max, 1)

                def take(it, s, chunks):
                    q2, h = divmod(s, GH)
                    u = (bg * QB + it * 2 + q2) * GH + h
                    for c in chunks:
                        if not dve_takes(s, c):
                            continue
                        dve.wait_ge(s_pt[c % 2], u * HC + c // 2 + 1 + (C_PT1 if c % 2 else 0))
                        dve.wait_ge(s_pv, u - 1 + C_PV)
                        v.tensor_copy(p_t[s % 2][:, c * 512:(c + 1) * 512], ps_p[c % 2][:]).then_inc(s_pe[c % 2], 1)

                def context(it, q2):
                    w = bg * QB + it * 2 + q2
                    link = Chain(dve, s_dl, w * 2)
                    dve.wait_ge(s_cxm, w + 1 + C_CXM)
                    sums = rsum[:, q2 * GH:(q2 + 1) * GH, :]
                    link(v.tensor_tensor(rinv[:, q2, :], sums[:, :, 0], sums[:, :, 1], ALU.add))
                    link(v.reciprocal(rinv[:, q2, :], rinv[:, q2, :]))
                    dve.wait_ge(s_st[q2], (bg * LOOPS + it) * 16 + C_ST)
                    v.tensor_tensor(cx_out[q2][:].rearrange("p (h d) -> p h d", h=GH),
                                    ps_c[q2][:, 0:GH * HD].rearrange("p (h d) -> p h d", h=GH),
                                    rinv[:, q2, :].unsqueeze(2).broadcast_to([P, GH, HD]), ALU.mult).then_inc(s_cxo, 1)

                def slots(it, first, final):
                    for s in range(RING):
                        nxt = (it + (s + 2) // RING, (s + 2) % RING)
                        scores(*nxt, 0)
                        take(it, s, range(HC))
                        scores(*nxt, 1)
                        if nxt[1] % GH == 1:
                            convert(nxt[0] + nxt[1] // GH, 1 - nxt[1] // GH)
                        take(it, s, range(HC, KC))
                        if s % GH == 2 and not (first and s < GH):
                            context(*((it - 1, 1) if s < GH else (it, 0)))
                    if final:
                        context(it, 1)

                if lead:
                    convert(0, 0)
                    for s in range(2):
                        scores(0, s, 0)
                        scores(0, s, 1)
                    convert(0, 1)
                    return
                slots(0, True, False)
                if LOOPS > 2:
                    with dve.Fori(1, LOOPS - 1) as it:
                        slots(it, False, False)
                slots(LOOPS - 1, False, True)

            emit(0, 0, 0, 0, lead=True)
            groups(dve, emit)



def ffn_stage(nc, net):
    B, S = net.B, net.S
    NB = S // TOK
    NT = B * NB
    with ExitStack() as ctx:
        def sb(name, shape, dt=F32):
            return ctx.enter_context(nc.sbuf_tensor(name, shape, dt))

        def sem(name):
            return ctx.enter_context(nc.semaphore(name))

        wo = sb("ff_wo", [P, DC, D])
        w1 = sb("ff_w1", [P, DC, FF])
        w2 = sb("ff_w2", [P, FC, D])
        bo = sb("ff_bo", [P, D])
        b1 = sb("ff_b1", [P, FC])
        b2 = sb("ff_b2", [P, D])
        g2 = sb("ff_g2", [P, D])
        beta2 = sb("ff_beta2", [P, D])
        minus_half = sb("ff_minus_half", [P, TJ])
        eps = sb("ff_eps", [P, TJ])
        cx = sb("ff_ctx", [P, TJ, D])
        x1 = sb("ff_x1", [P, TJ, D])
        t2 = sb("ff_cols", [P, DC, TOK])
        res = sb("ff_res", [P, TJ, D])
        hn = sb("ff_norm", [P, TJ, D])
        hn_t = sb("ff_norm_t", [P, DC, TOK])
        hid = sb("ff_hid", [P, FC, TOK])
        x2 = sb("ff_x2", [P, TJ, D])
        x3 = sb("ff_x3", [P, TJ, D])
        swap = sb("ff_swap", [P, D])
        feats = sb("ff_feats", [RANK, TOK])
        stats = sb("ff_stats", [P, TJ, 6])
        mv = sb("ff_mv", [P, TJ, 2])
        wait_cell = sb("ff_wait_cell", [P, 1])
        rstd = sb("ff_rstd", [P, TJ])

        ps_t = [ctx.enter_context(nc.psum_tensor(f"ff_ps_t{i}", [P, 512], F32)) for i in range(4)]
        ps_m = [ctx.enter_context(nc.psum_tensor(f"ff_ps_m{i}", [P, 512], F32)) for i in range(4)]

        s_w = sem("ff_weights_in")
        s_w1_in = sem("ff_w1_in")
        s_w2_in = sem("ff_w2_in")
        s_cx = sem("ff_ctx_in")
        s_x1 = sem("ff_x1_in")
        s_ct = sem("ff_ctx_transposed")
        s_ct_out = sem("ff_ctx_t_ready")
        s_wo = sem("ff_wo_done")
        s_res = sem("ff_res_ready")
        s_x1b = sem("ff_x1_bias_ready")
        s_mv = sem("ff_moments")
        s_rs = sem("ff_rstd_ready")
        s_n = sem("ff_norm_scaled")
        s_hn = sem("ff_norm_ready")
        s_x2 = sem("ff_x2_ready")
        s_ht = sem("ff_norm_transposed")
        s_ht_out = sem("ff_norm_t_ready")
        s_w1 = sem("ff_w1_done")
        s_gelu = sem("ff_gelu_ready")
        s_w2 = sem("ff_w2_done")
        s_x2w = sem("ff_w2_taken")
        s_x3 = sem("ff_x3_ready")
        s_acc = sem("ff_sums")
        s_xt = sem("ff_x3_transposed")
        s_xt_out = sem("ff_x3_t_ready")
        s_f = sem("ff_feats_done")
        s_f_out = sem("ff_feats_ready")
        s_link = sem("ff_dve_norm_steps")
        s_rot = sem("ff_dve_rotation_steps")
        s_plink = sem("ff_pool_steps")
        s_x3_st = sem("ff_x3_stored")
        s_f_st = sem("ff_feats_stored")
        n_w = 6

        def batch_of(n):
            return min(max(n - 1, 0), NT - 1) // NB

        def drive(eng, emit):
            rounds(eng, NT + 1, batch_of, 3, NT - 2, emit)

        block = ctx.enter_context(nc.Block())

        @block.sync
        def _(sp):
            cxv = net.ctx.rearrange("(t j p) d -> t p j d", j=TJ, p=P)
            x1v = net.x1.rearrange("(t j p) d -> t p j d", j=TJ, p=P)
            x3v = net.x3.rearrange("(t j p) d -> t p j d", j=TJ, p=P)
            fv = net.feats.rearrange("r (t n) -> t r n", n=TOK)
            sp.dma_start(cx[:], cxv[0]).then_inc(s_cx, 16)
            sp.dma_start(x1[:], x1v[0]).then_inc(s_x1, 16)
            sp.dma_start(wo[:], net.given["Wo"].rearrange("(c p) n -> p c n", p=P)).then_inc(s_w, 16)
            sp.dma_start(b1[:], net.given["b1"]).then_inc(s_w, 16)
            for to, v in ((bo, net.given["bo"]), (b2, net.given["b2"]), (g2, net.given["g2"]), (beta2, net.given["beta2"])):
                sp.dma_start(to[:], rows(v)).then_inc(s_w, 16)
            sp.dma_start(w1[:], net.given["W1"].rearrange("(c p) n -> p c n", p=P)).then_inc(s_w1_in, 16)
            sp.dma_start(w2[:], net.given["W2"].rearrange("(c p) n -> p c n", p=P)).then_inc(s_w2_in, 16)

            def emit(n, n0, b):
                if n0 >= 2:
                    sp.wait_ge(s_f_out, n - 1)
                    sp.dma_start(fv[n - 2], feats[:]).then_inc(s_f_st, 16)
                if n0 < NT - 1:
                    sp.wait_ge(s_ct, 4 * n + 4)
                    sp.dma_start(cx[:], cxv[n + 1]).then_inc(s_cx, 16)
                    sp.wait_ge(s_res, 4 * n + 4)
                    sp.dma_start(x1[:], x1v[n + 1]).then_inc(s_x1, 16)
                if n0 >= 1 and n0 <= NT:
                    sp.wait_ge(s_x3, 4 * n)
                    sp.dma_start(x3v[n - 1], x3[:]).then_inc(s_x3_st, 16)

            drive(sp, emit)
            sp.wait_ge(s_x3_st, 16 * NT)
            sp.wait_ge(s_f_st, 16 * NT)

        @block.tensor
        def _(pe):
            ident = net.consts[:, C_IDENT:C_IDENT + P]
            pe.wait_ge(s_w, 16 * n_w)

            def emit(n, n0, b):
                p, z = n - 1, n - 2
                front, middle, tail = n0 < NT, 1 <= n0 <= NT, n0 >= 2

                def to_columns(src, c, done):
                    for j in range(TJ):
                        last = pe.transpose(ps_t[c][:, j * P:(j + 1) * P], src[:, j, c * P:(c + 1) * P], ident)
                    last.then_inc(done, 1)

                def w1_groups(first):
                    for f in range(first, first + 8):
                        if f >= 12 or 4 <= f < 8:
                            pe.wait_ge(s_gelu, FC * p + f - 3)
                        elif f >= 8:
                            if front:
                                pe.wait_ge(s_res, 4 * n + f - 8 + 1)
                            else:
                                pe.wait_ge(s_gelu, FC * p + f - 3)
                                if tail and f == 8:
                                    pe.wait_ge(s_f_out, z + 1)
                        elif n0 >= 2:
                            pe.wait_ge(s_x2w, 4 * (p - 1) + f + 1)
                        for k in range(DC):
                            if f == 0:
                                pe.wait_ge(s_ht_out, 4 * p + k + 1)
                            last = pe.matmul(ps_m[f % 4][:], w1[:, k, f * P:(f + 1) * P], hn_t[:, k, :],
                                             start=(k == 0), stop=(k == DC - 1))
                        last.then_inc(s_w1, 1)

                if middle:
                    pe.wait_ge(s_hn, 4 * n)
                    for c in range(DC):
                        pe.wait_ge(s_ct_out, 4 * p + c + 1)
                        to_columns(hn, c, s_ht)
                    if n0 == 1:
                        pe.wait_ge(s_w1_in, 16)
                    w1_groups(0)
                if tail:
                    pe.wait_ge(s_x3, 4 * z + 4)
                    for c in range(DC):
                        if middle:
                            pe.wait_ge(s_ht_out, 4 * p + c + 1)
                        else:
                            pe.wait_ge(s_ht_out, 4 * z + c + 1)
                            pe.wait_ge(s_xt_out, 4 * (z - 1) + c + 1)
                        to_columns(x3, c, s_xt)
                    if middle:
                        pe.wait_ge(s_gelu, FC * p + 5)
                    else:
                        pe.wait_ge(s_x2w, 4 * z + 1)
                    for c in range(DC):
                        pe.wait_ge(s_xt_out, 4 * z + c + 1)
                        last = pe.matmul(ps_m[0][0:RANK, :], net.basis[:, c, :], t2[:, c, :],
                                         start=(c == 0), stop=(c == DC - 1))
                    last.then_inc(s_f, 1)
                if front:
                    pe.wait_ge(s_cx, 16 * (n + 1))
                    for c in range(DC):
                        if tail:
                            pe.wait_ge(s_xt_out, 4 * z + c + 1)
                        elif middle:
                            pe.wait_ge(s_ht_out, 4 * p + c + 1)
                        to_columns(cx, c, s_ct)
                    for j in range(TJ):
                        if tail and j == 0:
                            pe.wait_ge(s_f_out, z + 1)
                        if middle:
                            pe.wait_ge(s_gelu, FC * p + 4 + j + 1)
                        for k in range(DC):
                            pe.wait_ge(s_ct_out, 4 * n + k + 1)
                            last = pe.matmul(ps_m[j][:], t2[:, k, j * P:(j + 1) * P], wo[:, k, :],
                                             start=(k == 0), stop=(k == DC - 1))
                        last.then_inc(s_wo, 1)
                if middle:
                    w1_groups(8)
                    if n0 == 1:
                        pe.wait_ge(s_w2_in, 16)
                    for j in range(TJ):
                        pe.wait_ge(s_gelu, FC * p + 12 + j + 1)
                        for k in range(FC):
                            if j == 0 and k >= 12:
                                pe.wait_ge(s_gelu, FC * p + k + 1)
                            last = pe.matmul(ps_m[j][:], hid[:, k, j * P:(j + 1) * P], w2[:, k, :],
                                             start=(k == 0), stop=(k == FC - 1))
                        last.then_inc(s_w2, 1)

            drive(pe, emit)

        @block.scalar
        def _(act):
            act.wait_ge(s_w, 16 * n_w)

            def emit(n, n0, b):
                p, z = n - 1, n - 2
                front, middle, tail = n0 < NT, 1 <= n0 <= NT, n0 >= 2

                def gelus(first):
                    for f in range(first, first + 8):
                        act.wait_ge(s_w1, FC * p + f + 1)
                        if n0 >= 2 and f == 0:
                            act.wait_ge(s_w2, 4 * (p - 1) + 4)
                        act.activation(hid[:, f, :], ps_m[f % 4][:], ACT.Gelu_apprx_sigmoid,
                                       bias=b1[:, f:f + 1]).then_inc(s_gelu, 1)

                if middle:
                    for c in range(DC):
                        act.wait_ge(s_ht, 4 * p + c + 1)
                        if n0 >= 2:
                            act.wait_ge(s_w1, FC * p)
                        act.activation(hn_t[:, c, :], ps_t[c][:], ACT.Copy).then_inc(s_ht_out, 1)
                    gelus(0)
                if tail:
                    for c in range(DC):
                        act.wait_ge(s_xt, 4 * z + c + 1)
                        act.wait_ge(s_wo, 4 * min(z + 2, NT) if n0 > NT else 4 * (z + 2))
                        act.activation(t2[:, c, :], ps_t[c][:], ACT.Copy).then_inc(s_xt_out, 1)
                    act.wait_ge(s_f, z + 1)
                    if n0 >= 3:
                        act.wait_ge(s_f_st, 16 * z)
                    act.activation(feats[:], ps_m[0][0:RANK, :], ACT.Copy).then_inc(s_f_out, 1)
                if front:
                    for c in range(DC):
                        act.wait_ge(s_ct, 4 * n + c + 1)
                        if tail:
                            act.wait_ge(s_f, z + 1)
                        elif middle:
                            act.wait_ge(s_wo, 4 * n)
                        act.activation(t2[:, c, :], ps_t[c][:], ACT.Copy).then_inc(s_ct_out, 1)
                if middle:
                    gelus(8)

            drive(act, emit)

        @block.gpsimd
        def _(pool):
            step = Chain(pool, s_plink, 0)
            step(pool.memset(minus_half[:], -0.5))
            step(pool.memset(eps[:], LN_EPS))
            step(pool.memset(net.sums[:], 0.0))
            pool.wait_ge(s_w, 16 * n_w)

            def emit(n, n0, b):
                front, middle, tail = n0 < NT, 1 <= n0 <= NT, n0 >= 2
                if middle:
                    if n0 >= 2:
                        pool.wait_ge(s_x3, 4 * (n - 1))
                    pool.tensor_tensor(x2[:], res[:], b2[:].unsqueeze(1).broadcast_to([P, TJ, D]),
                                       ALU.add).then_inc(s_x2, 1)
                if front:
                    link = Chain(pool, s_plink, 3 + n)
                    pool.wait_ge(s_x1, 16 * (n + 1))
                    pool.tensor_tensor(x1[:], x1[:], bo[:].unsqueeze(1).broadcast_to([P, TJ, D]),
                                       ALU.add).then_inc(s_x1b, 1)
                    pool.wait_ge(s_mv, n + 1)
                    link(pool.tensor_tensor(rstd[:], mv[:, :, 1], eps[:], ALU.add))
                    pool.tensor_tensor(rstd[:], rstd[:], minus_half[:], ALU.pow).then_inc(s_rs, 1)
                    for j in range(TJ):
                        pool.wait_ge(s_n, 4 * n + j + 1)
                        pool.tensor_tensor(hn[:, j, :], hn[:, j, :], beta2[:], ALU.add).then_inc(s_hn, 1)
                if middle:
                    for j in range(TJ):
                        pool.wait_ge(s_x3, 4 * (n - 1) + j + 1)
                        pool.tensor_tensor(net.sums[:, b, :], net.sums[:, b, :], x3[:, j, :], ALU.add).then_inc(s_acc, 1)
                        pool.wait_ge(s_acc, 4 * (n - 1) + j + 1)

            drive(pool, emit)

        @block.vector
        def _(dve):
            v = nc.vector
            dve.wait_ge(s_w, 16 * n_w)

            def emit(n, n0, b):
                p, z = n - 1, n - 2
                front, middle, tail = n0 < NT, 1 <= n0 <= NT, n0 >= 2
                if front:
                    link = Chain(dve, s_link, n * (TJ + 1))
                    dve.wait_ge(s_x1b, n + 1)
                    if middle:
                        dve.wait_ge(s_x2, n)
                    for j in range(TJ):
                        dve.wait_ge(s_wo, 4 * n + j + 1)
                        v.tensor_tensor(res[:, j, :], ps_m[j][:], x1[:, j, :], ALU.add).then_inc(s_res, 1)
                    for j in range(TJ):
                        dve.wait_ge(s_res, 4 * n + j + 1)
                        last = v.bn_stats(stats[:, j, :], res[:, j, :])
                    link(last)
                    v.memset(wait_cell[:], 0.0)
                    for j in range(TJ):
                        last = v.bn_aggr(mv[:, j, :], stats[:, j, :])
                    last.then_inc(s_mv, 1)
                    dve.wait_ge(s_rs, n + 1)
                    if middle:
                        dve.wait_ge(s_ht, 4 * n)
                    for j in range(TJ):
                        link(v.tensor_scalar(hn[:, j, :], res[:, j, :], mv[:, j, 0:1], rstd[:, j:j + 1],
                                             ALU.subtract, ALU.mult))
                        v.tensor_tensor(hn[:, j, :], hn[:, j, :], g2[:], ALU.mult).then_inc(s_n, 1)
                if middle:
                    rot = Chain(dve, s_rot, p * 8)
                    dve.wait_ge(s_x2, p + 1)
                    if n0 >= 2:
                        dve.wait_ge(s_x3_st, 16 * p)
                        dve.wait_ge(s_acc, 4 * p)
                        dve.wait_ge(s_xt, 4 * p)
                    for j in range(TJ):
                        dve.wait_ge(s_w2, 4 * p + j + 1)
                        v.tensor_tensor(x2[:, j, :], ps_m[j][:], x2[:, j, :], ALU.add).then_inc(s_x2w, 1)
                        dve.wait_ge(s_x2w, 4 * p + j + 1)
                        x_sw = x2[:, j, :].rearrange("p (n f) -> p n f", f=2)[:, :, ::-1]
                        rot(v.tensor_tensor(swap[:].rearrange("p (n f) -> p n f", f=2), x_sw,
                                            net.rot_s[:, b, :].rearrange("p (n f) -> p n f", f=2), ALU.mult))
                        rot(v.tensor_tensor(x2[:, j, :], x2[:, j, :], net.rot_c[:, b, :], ALU.mult))
                        v.tensor_tensor(x3[:, j, :], x2[:, j, :], swap[:], ALU.add).then_inc(s_x3, 1)
                        dve.wait_ge(s_x3, 4 * p + j + 1)

            drive(dve, emit)



def output_stage(nc, net):
    B, S = net.B, net.S
    NB = S // TOK
    GH = D // 4
    BUFS = min(4, NB)
    TURNS = B * NB // BUFS
    C_Y = TJ
    with ExitStack() as ctx:
        def sb(name, shape, dt=F32):
            return ctx.enter_context(nc.sbuf_tensor(name, shape, dt))

        def sem(name):
            return ctx.enter_context(nc.semaphore(name))

        gw1 = sb("ou_gate_w1", [P, DC, GH])
        gb1 = sb("ou_gate_b1", [P, 1])
        gw2 = sb("ou_gate_w2", [P, 1])
        gb2 = sb("ou_gate_b2", [P, 1])
        safe = sb("ou_safety", [P, B])
        resp = sb("ou_resp", [RANK + 1, D])
        extra = sb("ou_resp_bias2", [RANK + 1, D])
        resp_s = sb("ou_resp_scaled", [RANK + 1, B, D])
        ones = sb("ou_ones", [P, P])
        pooled = sb("ou_pooled", [P, DC, B])
        h1 = sb("ou_h1", [P, B])
        act_in = sb("ou_act", [P, B])
        mod = sb("ou_mod", [P, B])
        strength = sb("ou_strength", [P, B])
        x3 = [sb(f"ou_x3_{i}", [P, TJ, D]) for i in range(BUFS)]
        ft = [sb(f"ou_feats{i}", [RANK + 1, TOK]) for i in range(BUFS)]

        ps_g = [ctx.enter_context(nc.psum_tensor(f"ou_ps_g{i}", [P, 512], F32)) for i in range(3)]
        ps_r = [ctx.enter_context(nc.psum_tensor(f"ou_ps_r{i}", [P, 512], F32)) for i in range(4)]

        s_w = sem("ou_weights_in")
        s_dve = sem("ou_dve_steps")
        s_ones = sem("ou_ones_ready")
        s_pool = sem("ou_pooled_done")
        s_h1 = sem("ou_h1_done")
        s_g = sem("ou_gate_done")
        s_pl = sem("ou_pooled_ready")
        s_hr = sem("ou_h1_ready")
        s_sig = sem("ou_sigmoids_ready")
        s_rs = sem("ou_resp_ready")
        s_x3 = [sem(f"ou_x3_in{i}") for i in range(BUFS)]
        s_ft = [sem(f"ou_feats_in{i}") for i in range(BUFS)]
        s_r = sem("ou_response_done")
        s_y = sem("ou_sum_ready")
        s_out = [sem(f"ou_stored{i}") for i in range(BUFS)]

        block = ctx.enter_context(nc.Block())

        @block.sync
        def _(sp):
            sp.dma_start(gw1[:], net.given["gate_w1T"].rearrange("(c p) j -> p c j", p=P)).then_inc(s_w, 16)
            sp.dma_start(gb1[:], net.given["gate_b1"].rearrange("(p a) -> p a", a=1)).then_inc(s_w, 16)
            sp.dma_start(gw2[:], net.given["gate_w2"].rearrange("a p -> p a")).then_inc(s_w, 16)
            sp.dma_start(gb2[:], rows(net.given["gate_b2"])).then_inc(s_w, 16)
            sp.dma_start(safe[:], rows(net.given["safety"])).then_inc(s_w, 16)
            sp.dma_start(resp[0:RANK, :], net.given["resp_wT"]).then_inc(s_w, 16)
            sp.dma_start(resp[RANK:RANK + 1, :], rows(net.given["resp_b"], 1)).then_inc(s_w, 16)
            sp.dma_start(extra[RANK:RANK + 1, :], rows(net.given["safety_bias"], 1)).then_inc(s_w, 16)
            x3v = net.x3.rearrange("(t j p) d -> t p j d", j=TJ, p=P)
            fv = net.feats.rearrange("r (t n) -> t r n", n=TOK)
            ov = net.out.rearrange("b (t j p) d -> (b t) p j d", j=TJ, p=P)
            sp.wait_ge(s_ones, 1)

            def load(t, i):
                sp.dma_start(x3[i][:], x3v[t]).then_inc(s_x3[i], 16)
                sp.dma_start(ft[i][0:RANK, :], fv[t]).then_inc(s_ft[i], 16)

            def store(m, more):
                for i in range(BUFS):
                    sp.wait_ge(s_y, (BUFS * m + i) * TJ + TJ + C_Y)
                    sp.dma_start(ov[BUFS * m + i], x3[i][:]).then_inc(s_out[i], 16)
                if more:
                    for i in range(BUFS):
                        sp.wait_ge(s_out[i], 16 * m + 16)
                        load(BUFS * (m + 1) + i, i)

            for i in range(BUFS):
                load(i, i)
            with sp.Fori(0, TURNS - 1) as m:
                store(m, True)
            store(TURNS - 1, False)
            for i in range(BUFS):
                sp.wait_ge(s_out[i], 16 * TURNS)

        @block.tensor
        def _(pe):
            pe.wait_ge(s_w, 8 * 16)
            pe.wait_ge(s_ones, 1)
            for b in range(B):
                for c in range(DC):
                    last = pe.matmul(ps_g[0][:, c * B + b:c * B + b + 1], net.sums[:, b, c * P:(c + 1) * P],
                                     ones[:, 0:1], start=True, stop=True)
            last.then_inc(s_pool, 1)
            pe.wait_ge(s_pl, 1)
            for c in range(DC):
                last = pe.matmul(ps_g[1][:, 0:B], gw1[:, c, :], pooled[:, c, :], start=(c == 0), stop=(c == DC - 1))
            last.then_inc(s_h1, 1)
            pe.wait_ge(s_hr, 1)
            pe.matmul(ps_g[2][:, 0:B], ones[:], h1[:], start=True, stop=True).then_inc(s_g, 1)
            pe.wait_ge(s_rs, 1)
            for b in range(B):
                with pe.Fori(b * NB // BUFS, (b + 1) * NB // BUFS) as m:
                    for i in range(BUFS):
                        pe.wait_ge(s_ft[i], 16 * m + 16)
                        for j in range(TJ):
                            pe.wait_ge(s_y, (BUFS * m + i - 1) * TJ + j + 1 + C_Y)
                            pe.matmul(ps_r[j][:], ft[i][:, j * P:(j + 1) * P], resp_s[:, b, :], start=True,
                                      stop=True).then_inc(s_r, 1)

        @block.scalar
        def _(act):
            act.wait_ge(s_w, 8 * 16)
            act.activation(mod[:], safe[:], ACT.Sigmoid).then_inc(s_sig, 1)
            act.wait_ge(s_g, 1)
            act.activation(act_in[:], ps_g[2][:, 0:B], ACT.Sigmoid, bias=gb2[:, 0:1]).then_inc(s_sig, 1)

        @block.vector
        def _(dve):
            v = nc.vector
            link = Chain(dve, s_dve, 0)
            v.nop().then_inc(s_y, C_Y)
            for i in range(BUFS):
                v.memset(ft[i][RANK:RANK + 1, :], 1.0)
            v.memset(ones[:], 1.0).then_inc(s_ones, 1)
            dve.wait_ge(s_w, 8 * 16)
            link(v.tensor_tensor(resp[RANK:RANK + 1, :], resp[RANK:RANK + 1, :], extra[RANK:RANK + 1, :], ALU.add))
            dve.wait_ge(s_pool, 1)
            v.tensor_scalar(pooled[:].rearrange("p c b -> p (c b)"), ps_g[0][:, 0:DC * B], 1.0 / S, None,
                            ALU.mult).then_inc(s_pl, 1)
            dve.wait_ge(s_h1, 1)
            link(v.tensor_scalar(h1[:], ps_g[1][:, 0:B], gb1[:, 0:1], 0.0, ALU.add, ALU.max))
            v.tensor_scalar(h1[:], h1[:], gw2[:, 0:1], None, ALU.mult).then_inc(s_hr, 1)
            dve.wait_ge(s_sig, 2)
            link(v.tensor_tensor(strength[:], act_in[:], mod[:], ALU.mult))
            for b in range(B):
                last = v.tensor_scalar(resp_s[:, b, :], resp[:], strength[0:RANK + 1, b:b + 1], None, ALU.mult)
            last.then_inc(s_rs, 1)
            with dve.Fori(0, TURNS) as m:
                for i in range(BUFS):
                    dve.wait_ge(s_x3[i], 16 * m + 16)
                    for j in range(TJ):
                        dve.wait_ge(s_r, (BUFS * m + i) * TJ + j + 1)
                        v.tensor_tensor(x3[i][:, j, :], ps_r[j][:], x3[i][:, j, :], ALU.add).then_inc(s_y, 1)


def build_program(nc, t, out):
    B, S = t["x"].shape[0], t["x"].shape[1]

    def scratch(name, shape, dt=F32):
        return nc.dram_tensor(name, shape, dt, kind="Internal").ap()

    with ExitStack() as ctx:
        def sb(name, shape, dt=F32):
            return ctx.enter_context(nc.sbuf_tensor(name, shape, dt))

        net = Parts()
        net.B = B
        net.S = S
        net.out = out
        net.given = t
        net.x1 = scratch("x1", [B * S, D])
        net.v = scratch("v", [B * S, D])
        net.ctx = scratch("ctx", [B * S, D])
        net.x3 = scratch("x3", [B * S, D])
        net.feats = scratch("feats", [RANK, B * S])
        net.q_hi = scratch("q_hi", [D, B * S])
        net.q_lo = scratch("q_lo", [D, B * S])
        net.k_hi = scratch("k_hi", [D, B * S])
        net.k_lo = scratch("k_lo", [D, B * S])
        net.consts = sb("consts", [P, C_COLS])
        net.ident_bf = sb("ident_bf", [P, P], BF16)
        net.rot_c = sb("rot_c", [P, B, D])
        net.rot_s = sb("rot_s", [P, B, D])
        net.ada_scale = sb("ada_scale", [P, B, D])
        net.ada_shift = sb("ada_shift", [P, B, D])
        net.exp_w = sb("exp_w", [P, B, P])
        net.exp_bias = sb("exp_bias", [P, B])
        net.basis = sb("basis", [P, DC, RANK])
        net.sums = sb("sums", [P, B, D])
        with ExitStack() as embed_ctx:
            em = embed_weights(nc, embed_ctx)
            setup_stage(nc, net, em)
            embed_stage(nc, net, em)
        attention_stage(nc, net)
        ffn_stage(nc, net)
        output_stage(nc, net)



def layout(inputs):
    a = {k: np.asarray(v) for k, v in inputs.items()}

    def flip(m):
        return np.ascontiguousarray(m.T)

    def columns(v):
        return flip(v.reshape(-1, P))

    return {
        "x": a["x"], "domain": a["itok_B_0_15"], "t_step": a["itok_B_34_63"],
        "bias": a["fside_Bx16xSxS_0"], "theta": a["condB_theta"], "phi": a["condB_phi"],
        "safety": a["condB_safetyscore"], "mask": a["mask_Bx1xSxS_bk0"],
        "down_WT": flip(a["L0_cond_down_W"]), "down_b": a["L0_cond_down_b"],
        "up_WT": flip(a["L0_cond_up_W"]), "up_b": a["L0_cond_up_b"],
        "expert_WT": np.ascontiguousarray(a["L0_cond_expert_W"].transpose(0, 2, 1)),
        "expert_bT": flip(a["L0_cond_expert_b"]), "domain_embT": flip(a["L0_cond_domain_emb"]),
        "ln_gamma": a["L0_cond_ln_gamma"], "ln_beta": a["L0_cond_ln_beta"],
        "W_ada": a["L1_cond_W_ada"], "b_ada": a["L1_cond_b_ada"],
        "Wq": a["L1_cond_Wq"], "bq": columns(a["L1_cond_bq"]), "Wk": a["L1_cond_Wk"], "bk": columns(a["L1_cond_bk"]),
        "Wv": a["L1_cond_Wv"], "bv": a["L1_cond_bv"], "Wo": a["L1_cond_Wo"], "bo": a["L1_cond_bo"],
        "W1": a["L1_cond_W1"], "b1": columns(a["L1_cond_b1"]), "W2": a["L1_cond_W2"], "b2": a["L1_cond_b2"],
        "g2": a["L1_cond_g2"], "beta2": a["L1_cond_beta2"],
        "U": a["L3_cond_U"], "V": a["L3_cond_V"], "safety_bias": a["L3_cond_safety_bias"],
        "gate_w1T": flip(a["L3_cond_gate_w1"]), "gate_b1": a["L3_cond_gate_b1"],
        "gate_w2": a["L3_cond_gate_w2"], "gate_b2": a["L3_cond_gate_b2"],
        "resp_wT": flip(a["L3_cond_resp_w"]), "resp_b": a["L3_cond_resp_b"],
        "shape_consts": shape_constants(),
    }


def kernel(**inputs):
    from concourse import bacc
    from concourse.bass_utils import run_bass_kernel_spmd

    nc = bacc.Bacc("TRN2", target_bir_lowering=False, num_devices=1)
    arrays = layout(inputs)
    t = {name: nc.dram_tensor(f"in_{name}", a.shape, mybir.dt.from_np(a.dtype), kind="ExternalInput").ap()
         for name, a in arrays.items()}
    shape = arrays["x"].shape
    out = nc.dram_tensor("out_0", shape, F32, kind="ExternalOutput").ap()
    build_program(nc, t, out)
    r = run_bass_kernel_spmd(nc, [{f"in_{name}": a for name, a in arrays.items()}], core_ids=[0])
    return r.results[0]["out_0"]
```
